# Optimizing a Trainium2 kernel written in Bass

```python
import numpy as np
import jax
import jax.numpy as jnp

def _softmax(x, axis=-1):
    return jax.nn.softmax(x, axis=axis)

def _gelu(x):
    return jax.nn.gelu(x, approximate=True)

def _silu(x):
    return jax.nn.silu(x)

def _sigmoid(x):
    return jax.nn.sigmoid(x)

def _layernorm(x, axis=-1, eps=1e-05):
    m = jnp.mean(x, axis=axis, keepdims=True)
    v = jnp.var(x, axis=axis, keepdims=True)
    return (x - m) / jnp.sqrt(v + eps)

def _scatter_add(tgt, idx, src, axis=0):
    return tgt.at[idx].add(src)

def _segment_sum(src, seg, n):
    return jax.ops.segment_sum(src, seg, n)
kernel_name = 'mk_gnn_ffn_d1_gnn_r8_e4b11d'

def setup_inputs(seed: int=0):
    np.random.seed(seed)
    _w = jnp.asarray

    def _rec_inputs():
        import jax
        import jax.numpy as jnp
        _gk = jax.random.key(seed)
        x = -0.0002117 + 1 * jax.random.normal(jax.random.fold_in(_gk, 1), (6250, 256), jnp.float32)
        src = jax.random.randint(jax.random.fold_in(_gk, 2), (100000,), 0, 6250, jnp.int32)
        dst = jnp.minimum((6250 * jax.random.uniform(jax.random.fold_in(_gk, 3), (100000,)) ** 2.0).astype(jnp.int32), 49999)
        _o = jnp.argsort(dst, stable=True)
        src = src[_o]
        dst = dst[_o]
        return (x, src, dst)
    x, src, dst = _rec_inputs()

    def _L0_gnn_setup():
        import jax, jax.numpy as jnp
        import numpy as np
        NEG = -1000.0
        SLOPE = 0.01
        N_NODES, N_EDGES, D_IN, D_OUT, N_HEADS = (12500, 200000, 256, 64, 4)
        key = jax.random.key(seed)
        k0, k1, k2, k3, k4 = jax.random.split(key, 5)
        h = jax.random.normal(k0, (N_NODES, D_IN), jnp.float32)
        src = jax.random.randint(k1, (N_EDGES,), 0, N_NODES)
        dst = jax.random.randint(k2, (N_EDGES,), 0, N_NODES)
        W = jax.random.normal(k3, (N_HEADS, D_IN, D_OUT), jnp.float32) / np.sqrt(D_IN)
        att = jax.random.normal(k4, (N_HEADS, 2 * D_OUT), jnp.float32) / np.sqrt(2.0 * D_OUT)
        return {'h': h, 'W': W, 'att': att, 'src': src, 'dst': dst}
    _L0_gnn_all = _L0_gnn_setup()
    _L0_gnn_in = {k: v for k, v in _L0_gnn_all.items() if k in ('W', 'att')}
    del _L0_gnn_all

    def _L0_ffn_setup():
        import jax, jax.numpy as jnp
        import numpy as np
        TOP_K = 2
        LN_EPS = 1e-05
        key = jax.random.key(seed)
        ks = jax.random.split(key, 8)
        B, S, D, E, H = (16, 1024, 256, 8, 1024)
        x = jax.random.normal(ks[0], (B, S, D), dtype=jnp.float32)
        Wr = jax.random.normal(ks[1], (D, E), dtype=jnp.float32) * 0.1
        br = jnp.zeros((E,), dtype=jnp.float32)
        ln_g = jnp.ones((E, D), dtype=jnp.float32)
        ln_b = jnp.zeros((E, D), dtype=jnp.float32)
        W1 = jax.random.normal(ks[2], (E, D, H), dtype=jnp.float32) * (1.0 / np.sqrt(D))
        b1 = jnp.zeros((E, H), dtype=jnp.float32)
        W2 = jax.random.normal(ks[3], (E, H, D), dtype=jnp.float32) * (1.0 / np.sqrt(H))
        b2 = jnp.zeros((E, D), dtype=jnp.float32)
        return {'x': x, 'Wr': Wr, 'br': br, 'ln_g': ln_g, 'ln_b': ln_b, 'W1': W1, 'b1': b1, 'W2': W2, 'b2': b2}
    _L0_ffn_all = _L0_ffn_setup()
    _L0_ffn_in = {k: v for k, v in _L0_ffn_all.items() if k in ('Wr', 'br', 'ln_g', 'ln_b', 'W1', 'b1', 'W2', 'b2')}
    del _L0_ffn_all
    return {'x': x, 'src': src, 'dst': dst, 'L0_gnn_W': _L0_gnn_in['W'], 'L0_gnn_att': _L0_gnn_in['att'], 'L0_ffn_Wr': _L0_ffn_in['Wr'], 'L0_ffn_br': _L0_ffn_in['br'], 'L0_ffn_ln_g': _L0_ffn_in['ln_g'], 'L0_ffn_ln_b': _L0_ffn_in['ln_b'], 'L0_ffn_W1': _L0_ffn_in['W1'], 'L0_ffn_b1': _L0_ffn_in['b1'], 'L0_ffn_W2': _L0_ffn_in['W2'], 'L0_ffn_b2': _L0_ffn_in['b2']}

def reference(x, src, dst, L0_gnn_W, L0_gnn_att, L0_ffn_Wr, L0_ffn_br, L0_ffn_ln_g, L0_ffn_ln_b, L0_ffn_W1, L0_ffn_b1, L0_ffn_W2, L0_ffn_b2):
    import jax
    import jax.numpy as jnp

    def _L0_gnn_ref(h, W, att, src, dst):
        import jax, jax.numpy as jnp
        import numpy as np
        NEG = -1000.0
        SLOPE = 0.01
        N_NODES, N_EDGES, D_IN, D_OUT, N_HEADS = (12500, 200000, 256, 64, 4)
        N = h.shape[0]
        H, _, F = W.shape
        z = jnp.einsum('nd,hdf->nhf', h, W)
        a_src, a_dst = (att[:, :F], att[:, F:])
        es = jnp.einsum('nhf,hf->nh', z, a_src)
        ed = jnp.einsum('nhf,hf->nh', z, a_dst)
        e = jax.nn.leaky_relu(es[src] + ed[dst], SLOPE)
        e = jnp.where(e == 0.0, NEG, e)
        m = jax.ops.segment_max(e, dst, num_segments=N)
        m = jnp.where(jnp.isfinite(m), m, 0.0)
        ex = jnp.exp(e - m[dst])
        denom = jax.ops.segment_sum(ex, dst, num_segments=N)
        safe = jnp.where(denom[dst] > 0.0, denom[dst], 1.0)
        alpha = ex / safe
        out = jax.ops.segment_sum(alpha[:, :, None] * z[src], dst, num_segments=N)
        return out.reshape(N, H * F)

    def _L0_ffn_ref(x, Wr, br, ln_g, ln_b, W1, b1, W2, b2):
        import jax, jax.numpy as jnp
        import numpy as np
        TOP_K = 2
        LN_EPS = 1e-05
        B, S, D = x.shape
        N = B * S
        xt = x.reshape(N, D)
        logits = xt @ Wr + br
        probs = jax.nn.softmax(logits, axis=-1)
        top_p, top_idx = jax.lax.top_k(probs, TOP_K)
        weights = top_p / top_p.sum(axis=-1, keepdims=True)
        mu = xt.mean(axis=-1, keepdims=True)
        var = ((xt - mu) ** 2).mean(axis=-1, keepdims=True)
        xn = (xt - mu) * jax.lax.rsqrt(var + LN_EPS)
        xe = xn[None, :, :] * ln_g[:, None, :] + ln_b[:, None, :]
        h = jax.nn.gelu(jnp.einsum('end,edh->enh', xe, W1) + b1[:, None, :], approximate=False)
        y = jnp.einsum('enh,ehd->end', h, W2) + b2[:, None, :]
        y_tok = jnp.transpose(y, (1, 0, 2))
        sel = jnp.take_along_axis(y_tok, top_idx[:, :, None], axis=1)
        out = (weights[:, :, None] * sel).sum(axis=1)
        return out.reshape(B, S, D)
    x = x + _L0_gnn_ref(_layernorm(x, axis=-1), L0_gnn_W, L0_gnn_att, src, dst)
    x = x + _L0_ffn_ref(_layernorm(x, axis=-1)[None], L0_ffn_Wr, L0_ffn_br, L0_ffn_ln_g, L0_ffn_ln_b, L0_ffn_W1, L0_ffn_b1, L0_ffn_W2, L0_ffn_b2)[0]
    return x

_drawn_inputs = setup_inputs


def setup_inputs(seed=0):
    import zlib

    import numpy as np

    out = dict(_drawn_inputs(seed))
    spreads = {'L0_ffn_br': (0.0, 0.1),
     'L0_ffn_ln_g': (1.0, 0.2),
     'L0_ffn_ln_b': (0.0, 0.1),
     'L0_ffn_b1': (0.0, 0.1),
     'L0_ffn_b2': (0.0, 0.1)}
    factors = {}
    for name, (base, spread) in spreads.items():
        noise = np.random.default_rng([zlib.crc32(name.encode()), seed]).standard_normal(out[name].shape)
        drawn = base * np.exp(spread * noise) if base else spread * noise
        out[name] = jnp.asarray(drawn.astype(out[name].dtype))
    for name, factor in factors.items():
        out[name] = (out[name] * factor).astype(out[name].dtype)
    return out
```

```python
from contextlib import ExitStack

import concourse.bass as bass
from concourse import mybir
from concourse.alu_op_type import AluOpType as ALU

ACT = mybir.ActivationFunctionType
F32 = mybir.dt.float32
F16 = mybir.dt.float16
I32 = mybir.dt.int32
AX = mybir.AxisListType

P = 128
D = 256
KD = D // P
HEADS = 4
FH = D // HEADS
ZW = D + HEADS
NODES = 6250
NT = -(-NODES // P)
TAIL = NODES - (NT - 1) * P
EDGES = 100000
EC = 784
FULLP = EDGES // EC
ETAIL = EDGES - FULLP * EC
ETILES = EC
VISITS = 832
VB = 7
FAR = -1.0e30
NEG = -1000.0
SLOPE = 0.01
EPS = 1e-5
NE = 8
HID = 1024
MH = HID // P
ETL = -(-((2 * NODES + NE * (P - 1)) // P) // 6) * 6
SC = 64.0


class Tally:

    def __init__(self):
        self.n = 0

    def one(self):
        self.n += 1
        return 1


def constants(nc, K):
    with ExitStack() as ctx:
        ramp = ctx.enter_context(nc.sbuf_tensor("ramp", [P, P], I32))
        zeroed = ctx.enter_context(nc.semaphore("zeroed"))
        ramped = ctx.enter_context(nc.semaphore("ramped"))
        block = ctx.enter_context(nc.Block())

        @block.gpsimd
        def _(pool):
            pool.memset(K["ident"][:, :], 0.0).then_inc(zeroed, 1)
            pool.memset(K["ones"][:, :], 1.0)
            pool.memset(K["slot"][:, :, :], 0)
            pool.iota(ramp[:, :], pattern=[[1, P]], base=0, channel_multiplier=0).then_inc(ramped, 1)
            pool.wait_ge(zeroed, 1)
            pool.affine_select(out=K["ident"][:, :], in_=K["ident"][:, :], compare_op=ALU.not_equal,
                               fill=1.0, base=0, pattern=[[-1, P]], channel_multiplier=1)

        @block.vector
        def _(dve):
            dve.wait_ge(ramped, 1)
            dve.tensor_copy(K["iota"][:, :], ramp[:, :])


def project_nodes(nc, K, x, W, att, zt, es_tab, ed_tab):
    C = 7
    with ExitStack() as ctx:
        def sb(name, shape, dt=F32):
            return ctx.enter_context(nc.sbuf_tensor(name, shape, dt))

        def sem(name):
            return ctx.enter_context(nc.semaphore(name))

        X = K["x2"]
        wz = sb("wz", [P, KD, D + 2 * HEADS])
        attb = sb("attb", [P, HEADS, 2 * FH])
        watt = sb("watt", [P, KD, HEADS, 2, FH])
        stats = sb("stats", [P, C, 6])
        mv = sb("mv", [P, C, 2])
        vinv = sb("vinv", [P, C])
        rstd = sb("rstd", [P, C])
        xn = sb("xn", [P, C, D])
        xT = sb("xT", [P, C, D])
        zsb = sb("zsb", [P, C, D + 2 * HEADS])
        tps = [ctx.enter_context(nc.psum_tensor(f"tps{b}", [P, 512], F32)) for b in range(2)]
        zps = [ctx.enter_context(nc.psum_tensor(f"zps{b}", [P, 512], F32)) for b in range(2)]
        x_cleared = sem("x_cleared")
        x_in = sem("x_in")
        w_in = sem("w_in")
        wz_done = sem("wz_done")
        ln_step = sem("ln_step")
        root = sem("root")
        begun = sem("aggregation_begun")
        xn_ready = sem("xn_ready")
        turned = sem("turned")
        xT_ready = sem("xT_ready")
        z_ready = sem("z_ready")
        z_out = sem("z_out")
        z_stored = sem("z_stored")
        block = ctx.enter_context(nc.Block())

        @block.sync
        def _(sp):
            for k in range(KD):
                sp.dma_start(wz[:, k, 0:D].rearrange("p (h f) -> p h f", h=HEADS),
                             W[:, k * P:(k + 1) * P, :].rearrange("h p f -> p h f")).then_inc(w_in, 16)
            sp.dma_start(attb[:, :, :], att.partition_broadcast(P)).then_inc(w_in, 16)
            for c in range(6):
                sp.dma_start(X[:, 8 * c:8 * c + 8, :],
                             x[8 * c * P:8 * (c + 1) * P, :].rearrange("(t p) d -> p t d", p=P)).then_inc(x_in, 16)
            sp.wait_ge(x_cleared, 1)
            sp.dma_start(X[0:TAIL, NT - 1, :], x[(NT - 1) * P:NODES, :]).then_inc(x_in, 16)
            with sp.Fori(0, NT // C) as c:
                sp.wait_ge(z_out, c * C + C)
                rows = slice(c * C * P, (c + 1) * C * P)
                sp.dma_start(zt[bass.ds(c * (C * P), C * P), :].rearrange("(t p) d -> p t d", p=P),
                             zsb[:, :, 0:D]).then_inc(z_stored, 16)
                sp.dma_start(es_tab[bass.ds(c * (C * P), C * P), :].rearrange("(t p) d -> p t d", p=P),
                             zsb[:, :, D:D + HEADS]).then_inc(z_stored, 16)
                sp.dma_start(ed_tab[bass.ds(c * (C * P), C * P), :].rearrange("(t p) d -> p t d", p=P),
                             zsb[:, :, D + HEADS:D + 2 * HEADS]).then_inc(z_stored, 16)
            sp.wait_ge(z_stored, 48 * (NT // C))

        @block.vector
        def _(dve):
            dve.memset(X[:, NT - 1, :], 0.0).then_inc(x_cleared, 1)
            dve.wait_ge(w_in, 16 * (KD + 1))
            for k in range(KD):
                for side in range(2):
                    dve.tensor_tensor(watt[:, k, :, side, :],
                                      wz[:, k, 0:D].rearrange("p (h f) -> p h f", h=HEADS),
                                      attb[:, :, side * FH:(side + 1) * FH], ALU.mult).then_inc(wz_done, 1)
            dve.wait_ge(wz_done, 4)
            for k in range(KD):
                for side in range(2):
                    dve.tensor_reduce(wz[:, k, D + side * HEADS:D + (side + 1) * HEADS],
                                      watt[:, k, :, side, :], AX.X, ALU.add).then_inc(wz_done, 1)
            dve.wait_ge(x_in, 16 * 7)
            with dve.Fori(0, NT // C) as c:
                dve.wait_ge(xn_ready, c * C)
                for j in range(C):
                    dve.bn_stats(stats[:, j, :], X[:, c * C + j, :]).then_inc(ln_step, 1)
                dve.wait_ge(ln_step, c * (2 * C + 2) + C)
                dve.sem_inc(begun, 1)
                for j in range(C):
                    dve.bn_aggr(mv[:, j, :], stats[:, j, :]).then_inc(ln_step, 1)
                dve.wait_ge(ln_step, c * (2 * C + 2) + 2 * C)
                dve.tensor_scalar(vinv[:, :], mv[:, :, 1], EPS, None, ALU.add).then_inc(ln_step, 1)
                dve.wait_ge(ln_step, c * (2 * C + 2) + 2 * C + 1)
                dve.reciprocal(vinv[:, :], vinv[:, :]).then_inc(ln_step, 1)
                dve.wait_ge(root, c + 1)
                for j in range(C):
                    dve.wait_ge(turned, c * C + j + 1)
                    dve.tensor_scalar(xn[:, j, :], X[:, c * C + j, :], mv[:, j, 0:1], rstd[:, j:j + 1],
                                      ALU.subtract, ALU.mult).then_inc(xn_ready, 1)

        @block.scalar
        def _(act):
            with act.Fori(0, NT // C) as c:
                act.wait_ge(ln_step, c * (2 * C + 2) + 2 * C + 2)
                act.activation(rstd[:, :], vinv[:, :], ACT.Sqrt).then_inc(root, 1)
                act.wait_ge(z_stored, c * 48)
                for j in range(C + 1):
                    if j < C:
                        act.wait_ge(turned, c * C + j + 1 + C)
                        act.activation(xT[:, j, :], tps[j % 2][:, 0:D], ACT.Copy).then_inc(xT_ready, 1)
                    if j >= 1:
                        act.wait_ge(z_ready, c * C + j)
                        act.activation(zsb[:, j - 1, :], zps[(j - 1) % 2][:, 0:D + 2 * HEADS],
                                       ACT.Copy).then_inc(z_out, 1)

        @block.tensor
        def _(pe):
            pe.sem_inc(turned, C)
            pe.wait_ge(wz_done, 8)

            def project(c, j):
                pe.wait_ge(xT_ready, c * C + j + 1)
                pe.wait_ge(z_out, c * C + j - 1 if j else c * C)
                for k in range(KD):
                    mm = pe.matmul(zps[j % 2][:, 0:D + 2 * HEADS], xT[:, j, k * P:(k + 1) * P], wz[:, k, :],
                                   start=(k == 0), stop=(k == KD - 1))
                mm.then_inc(z_ready, 1)

            with pe.Fori(0, NT // C) as c:
                for j in range(C):
                    pe.wait_ge(xn_ready, c * C + j + 1)
                    pe.wait_ge(xT_ready, c * C + j - 1 if j else c * C)
                    for k in range(KD):
                        mm = pe.transpose(tps[j % 2][:, k * P:(k + 1) * P], xn[:, j, k * P:(k + 1) * P],
                                          K["ident"][:, :])
                    mm.then_inc(turned, 1)
                    if j >= 1:
                        project(c, j - 1)
                project(c, C - 1)


def edge_scores(nc, K, src, dst, es_tab, ed_tab, rec):
    G = 8
    NG = EC // G
    with ExitStack() as ctx:
        def sb(name, shape, dt=F32):
            return ctx.enter_context(nc.sbuf_tensor(name, shape, dt))

        def sem(name):
            return ctx.enter_context(nc.semaphore(name))

        srcI = sb("srcI", [P, EC + 2 * G], I32)
        dstI = sb("dstI", [P, EC + 2 * G], I32)
        edge0 = sb("edge0", [P, 2], I32)
        pad = sb("pad", [P, EC])
        srcF = sb("srcF", [P, EC])
        dstF = sb("dstF", [P, EC])
        before = sb("before", [P, EC])
        after = sb("after", [P, EC])
        idx = sb("idx", [P, 2, 2, G], I32)
        got = sb("got", [P, 2, 2, G, HEADS])
        es = sb("es", [P, HEADS, EC])
        ed = sb("ed", [P, HEADS, EC])
        run = sb("run", [P, HEADS, EC])
        joined = sb("joined", [P, 4])
        ends = sb("ends", [P, 2, 2, HEADS])
        rows = sb("rows", [HEADS, 2, 2, P])
        carried = sb("carried", [HEADS, 2, P + 1])
        first = sb("first", [P, 2, HEADS])
        below = sb("below", [P, EC])
        cps = [ctx.enter_context(nc.psum_tensor(f"cps{b}", [P, 512], F32)) for b in range(3)]
        filled = sem("filled")
        edges_in = sem("edges_in")
        prep = sem("prep")
        edge_no = sem("edge_no")
        idx_ready = sem("idx_ready")
        landed = [sem(f"landed{s}") for s in range(2)]
        got_out = sem("got_out")
        math = sem("math")
        begun = sem("groups_begun")
        counted = sem("counted")
        turned = sem("ends_turned")
        exped = sem("exped")
        rec_out = sem("rec_out")
        block = ctx.enter_context(nc.Block())

        @block.sync
        def _(sp):
            sp.wait_ge(filled, 4)
            for tile, edges in ((srcI, src), (dstI, dst)):
                sp.dma_start(tile[0:FULLP, 0:EC], edges[0:FULLP * EC].rearrange("(p t) -> p t", t=EC)).then_inc(edges_in, 16)
                sp.dma_start(tile[FULLP:P, 0:ETAIL], edges[FULLP * EC:EDGES].rearrange("(p t) -> p t", t=ETAIL)).then_inc(edges_in, 16)
            ahead = dst[0:FULLP * EC].rearrange("(p t) -> p t", t=EC)
            sp.dma_start(edge0[1:P, 0:1], ahead[:, EC - 1:EC], allow_slow_non_contiguous=True).then_inc(edges_in, 16)
            sp.dma_start(edge0[0:FULLP - 1, 1:2], ahead[1:FULLP, 0:1], allow_slow_non_contiguous=True).then_inc(edges_in, 16)
            sp.dma_start(edge0[FULLP - 1:FULLP, 1:2], dst[FULLP * EC:FULLP * EC + 1].rearrange("(p t) -> p t", t=1)).then_inc(edges_in, 16)
            sp.wait_ge(prep, 3)
            sp.wait_ge(counted, 1)
            sp.dma_start(rec[0, :].rearrange("(p t) -> p t", t=EC), srcF[:, :]).then_inc(rec_out, 16)
            sp.dma_start(rec[1, :].rearrange("(p t) -> p t", t=EC), dstF[:, :]).then_inc(rec_out, 16)
            for h in range(HEADS):
                sp.wait_ge(exped, h + 1)
                sp.dma_start(rec[2 + h, :].rearrange("(p t) -> p t", t=EC), es[:, h, :]).then_inc(rec_out, 16)
            sp.wait_ge(rec_out, 16 * 6)

        @block.gpsimd
        def _(pool):
            pool.memset(srcI[:, :], 0).then_inc(filled, 1)
            pool.memset(dstI[:, :], 0).then_inc(filled, 1)
            pool.memset(edge0[:, :], -1).then_inc(filled, 1)
            pool.iota(pad[:, :].bitcast(I32), pattern=[[1, EC]], base=0, channel_multiplier=EC).then_inc(filled, 1)
            with pool.Fori(0, NG // 2) as i:
                for s in range(2):
                    pool.wait_ge(idx_ready, 4 * i + 2 * s + 2)
                    pool.sem_inc(begun, 1)
                    for side, table in enumerate((es_tab, ed_tab)):
                        for g in range(G):
                            pool.indirect_dma_start(
                                out=got[:, s, side, g, :], out_offset=None, in_=table[:, :],
                                in_offset=bass.IndirectOffsetOnAxis(ap=idx[:, s, side, g:g + 1], axis=0)).then_inc(landed[s], 16)

        @block.vector
        def _(dve):
            n = Tally()
            dve.wait_ge(edges_in, 16 * 7)
            dve.wait_ge(filled, 4)

            def indices(start, s):
                dve.tensor_copy(idx[:, s, 0, :], srcI[:, bass.ds(start, G)]).then_inc(idx_ready, 1)
                dve.tensor_copy(idx[:, s, 1, :], dstI[:, bass.ds(start, G)]).then_inc(idx_ready, 1)

            for s in range(2):
                indices(s * G, s)
            dve.tensor_copy(below[:, :], pad[:, :].bitcast(I32)).then_inc(prep, 1)
            dve.tensor_copy(srcF[:, :], srcI[:, 0:EC]).then_inc(counted, 1)
            dve.wait_ge(prep, 1)
            dve.tensor_scalar(below[:, :], below[:, :], float(EDGES), 8192.0, ALU.is_ge, ALU.mult).then_inc(prep, 1)
            dve.wait_ge(prep, 2)
            dve.tensor_tensor(dstF[:, :], dstI[:, 0:EC], below[:, :], ALU.add).then_inc(prep, 1)
            dve.wait_ge(prep, 3)
            dve.tensor_tensor(before[:, 1:EC], dstF[:, 1:EC], dstF[:, 0:EC - 1], ALU.not_equal).then_inc(prep, 1)
            dve.tensor_tensor(before[:, 0:1], dstF[:, 0:1], edge0[:, 0:1], ALU.not_equal).then_inc(prep, 1)
            dve.tensor_tensor(after[:, 0:EC - 1], dstF[:, 1:EC], dstF[:, 0:EC - 1], ALU.not_equal).then_inc(prep, 1)
            dve.tensor_tensor(after[:, EC - 1:EC], dstF[:, EC - 1:EC], edge0[:, 1:2], ALU.not_equal).then_inc(prep, 1)
            dve.tensor_tensor(joined[:, 0:1], dstF[:, 0:1], dstF[:, EC - 1:EC], ALU.not_equal).then_inc(prep, 1)
            dve.wait_ge(prep, 8)
            dve.tensor_tensor(joined[:, 1:2], joined[:, 0:1], before[:, 0:1], ALU.max).then_inc(prep, 1)
            dve.tensor_tensor(joined[:, 2:3], joined[:, 0:1], after[:, EC - 1:EC], ALU.max).then_inc(prep, 1)
            dve.wait_ge(prep, 10)
            dve.tensor_scalar(before[:, :], before[:, :], FAR, None, ALU.mult).then_inc(prep, 1)
            dve.tensor_scalar(after[:, :], after[:, :], FAR, None, ALU.mult).then_inc(prep, 1)
            for d in range(2):
                for h in range(HEADS):
                    dve.tensor_scalar(ends[:, d, 1, h:h + 1], joined[:, 1 + d:2 + d], FAR, None, ALU.mult).then_inc(prep, 1)
            dve.memset(K["counts"][:, 0:1], 0.0)
            dve.memset(K["counts"][:, NT:NT + 1], EDGES / P)
            for w in range(1, NT):
                dve.tensor_scalar(below[:, :], dstF[:, :], float(P * w), 0.0, ALU.is_lt, ALU.add,
                                  accum_out=K["counts"][:, w:w + 1]).then_inc(counted, 1)
                dve.wait_ge(counted, w + 1)

            with dve.Fori(0, NG // 2) as i:
                for s in range(2):
                    dve.wait_ge(landed[s], (i + 1) * (2 * G * 16))
                    at = (2 * i + s) * G
                    dve.tensor_copy(es[:, :, bass.ds(at, G)].rearrange("p h g -> p g h"), got[:, s, 0, :, :]).then_inc(got_out, 1)
                    dve.tensor_copy(ed[:, :, bass.ds(at, G)].rearrange("p h g -> p g h"), got[:, s, 1, :, :]).then_inc(got_out, 1)
                    dve.wait_ge(got_out, 4 * i + 2 * s + 2)
                    indices(at + 2 * G, s)
            dve.wait_ge(got_out, 2 * NG)

            dve.tensor_tensor(es[:, :, :], es[:, :, :], ed[:, :, :], ALU.add).then_inc(math, n.one())
            dve.wait_ge(math, n.n)
            dve.scalar_tensor_tensor(out=es[:, :, :], in0=es[:, :, :], scalar=SLOPE, in1=es[:, :, :],
                                     op0=ALU.mult, op1=ALU.max).then_inc(math, n.one())
            dve.wait_ge(math, n.n)
            dve.tensor_scalar(ed[:, :, :], es[:, :, :], 0.0, NEG, ALU.is_equal, ALU.mult).then_inc(math, n.one())
            dve.wait_ge(math, n.n)
            dve.tensor_tensor(es[:, :, :], es[:, :, :], ed[:, :, :], ALU.add).then_inc(math, n.one())
            dve.wait_ge(math, n.n)
            for d in range(2):
                step = 1 if d == 0 else -1
                keep = (before, after)[d]
                data, out = ((es, run), (run, ed))[d]
                for h in range(HEADS):
                    dve.tensor_tensor_scan(out[:, h, ::step], keep[:, ::step], data[:, h, ::step], FAR,
                                           ALU.add, ALU.max).then_inc(math, n.one())
                dve.wait_ge(math, n.n)
                end = EC - 1 if d == 0 else 0
                dve.tensor_copy(ends[:, d, 0, :], out[:, :, end]).then_inc(math, n.one())
                K["ends_at"][d] = n.n
                dve.memset(carried[:, d, :], FAR).then_inc(math, n.one())
                dve.wait_ge(turned, 2 * d + 1)
                dve.tensor_copy(rows[:, d, 0, :], cps[0][0:HEADS, 0:P]).then_inc(math, n.one())
                dve.tensor_copy(rows[:, d, 1, :], cps[1][0:HEADS, 0:P]).then_inc(math, n.one())
                dve.wait_ge(math, n.n)
                at = slice(1, P + 1) if d == 0 else slice(P - 1, None, -1)
                dve.tensor_tensor_scan(carried[:, d, at], rows[:, d, 1, ::step], rows[:, d, 0, ::step], FAR,
                                       ALU.add, ALU.max).then_inc(math, n.one())
                K["carried_at"][d] = n.n
                dve.wait_ge(turned, 2 * d + 2)
                dve.tensor_copy(first[:, d, :], cps[2][:, 0:HEADS]).then_inc(math, n.one())
                dve.wait_ge(math, n.n)
                for h in range(HEADS):
                    dve.tensor_tensor_scan(out[:, h, ::step], keep[:, ::step], data[:, h, ::step],
                                           first[:, d, h:h + 1], ALU.add, ALU.max).then_inc(math, n.one())
                dve.wait_ge(math, n.n)
            dve.tensor_tensor(run[:, :, :], es[:, :, :], ed[:, :, :], ALU.subtract).then_inc(math, n.one())
            K["math_end"] = n.n

        @block.tensor
        def _(pe):
            for d in range(2):
                pe.wait_ge(prep, 20)
                pe.wait_ge(math, K["ends_at"][d])
                pe.transpose(cps[0][0:HEADS, 0:P], ends[:, d, 0, :], K["ident"][:, :])
                pe.transpose(cps[1][0:HEADS, 0:P], ends[:, d, 1, :], K["ident"][:, :]).then_inc(turned, 1)
                pe.wait_ge(math, K["carried_at"][d])
                at = slice(0, P) if d == 0 else slice(1, P + 1)
                pe.transpose(cps[2][:, 0:HEADS], carried[:, d, at], K["ident"][0:HEADS, 0:HEADS]).then_inc(turned, 1)

        @block.scalar
        def _(act):
            act.wait_ge(math, K["math_end"])
            for h in range(HEADS):
                act.activation(es[:, h, :], run[:, h, :], ACT.Exp).then_inc(exped, 1)


def plan_visits(nc, K, rec, wtab):
    with ExitStack() as ctx:
        def sb(name, shape, dt=F32):
            return ctx.enter_context(nc.sbuf_tensor(name, shape, dt))

        def sem(name):
            return ctx.enter_context(nc.semaphore(name))

        start = sb("start", [P, NT + 1])
        startI = sb("startI", [P, 2, NT + 1], I32)
        tiles = sb("tiles", [P, 2, NT + 1])
        many = sb("many", [P, NT])
        vend = sb("vend", [P, NT])
        zero = sb("zero", [P, NT])
        shift = sb("shift", [P, NT])
        vI = sb("vI", [P, VB], I32)
        v = sb("v", [P, VB])
        mask = sb("mask", [P, VB, NT])
        wv = sb("wv", [P, VB])
        w0 = sb("w0", [P, VB])
        wI = sb("wI", [P, VB], I32)
        tv = sb("tv", [P, VB])
        tI = sb("tI", [P, 6, VB], I32)
        tF = sb("tF", [P, 6, VB])
        vr = sb("vr", [P, 6, VB, P])
        sps = ctx.enter_context(nc.psum_tensor("sps", [P, 512], F32))
        vps = [ctx.enter_context(nc.psum_tensor(f"vps{b}", [P, 512], F32)) for b in range(4)]
        ramp = sem("v_ramp")
        sums = sem("sums")
        step = sem("plan_step")
        planned = sem("planned")
        fetched = sem("fetched")
        local = sem("local")
        turned = sem("visits_turned")
        laid = sem("laid")
        table = sem("table")
        block = ctx.enter_context(nc.Block())

        @block.gpsimd
        def _(pool):
            pool.iota(vI[:, :], pattern=[[P, VB]], base=0, channel_multiplier=1).then_inc(ramp, 1)
            pool.wait_ge(planned, 1)
            for k in range(6):
                for b in range(VB):
                    pool.indirect_dma_start(
                        out=vr[:, k, b, :], out_offset=None, in_=rec.rearrange("k (t e) -> (k t) e", e=P),
                        in_offset=bass.IndirectOffsetOnAxis(ap=tI[:, k, b:b + 1], axis=0)).then_inc(fetched, 16)

        @block.tensor
        def _(pe):
            pe.matmul(sps[:, 0:NT + 1], K["ones"][:, :], K["counts"][:, :], start=True, stop=True).then_inc(sums, 1)
            pe.wait_ge(fetched, 16 * 6 * VB)
            pe.wait_ge(local, VB)
            for k in range(6):
                for b in range(VB):
                    m = k * VB + b
                    if m >= 4:
                        pe.wait_ge(laid, m - 3)
                    pe.transpose(vps[m % 4][:, 0:P], vr[:, k, b, :], K["ident"][:, :]).then_inc(turned, 1)

        @block.scalar
        def _(act):
            for m in range(6 * VB):
                k, b = m // VB, m % VB
                act.wait_ge(turned, m + 1)
                to = (K["srcV"], K["dstV"])[k][:, b * P:(b + 1) * P] if k < 2 else K["exV"][:, b * P:(b + 1) * P, k - 2]
                act.activation(to, vps[m % 4][:, 0:P], ACT.Copy).then_inc(laid, 1)

        @block.sync
        def _(sp):
            sp.wait_ge(planned, 1)
            sp.dma_start(wtab.rearrange("(b p) -> p b", p=P), wI[:, :], allow_slow_non_contiguous=True).then_inc(table, 16)
            sp.wait_ge(table, 16)
            sp.dma_start(K["wrow"][:, :], wtab.rearrange("(a v) -> a v", a=1)).then_inc(table, 16)
            sp.wait_ge(table, 32)

        @block.vector
        def _(dve):
            n = Tally()

            def after(ins):
                ins.then_inc(step, n.one())
                dve.wait_ge(step, n.n)

            after(dve.memset(zero[:, :], 0.0))
            dve.wait_ge(ramp, 1)
            after(dve.tensor_copy(v[:, :], vI[:, :]))
            dve.wait_ge(sums, 1)
            after(dve.tensor_copy(start[:, :], sps[:, 0:NT + 1]))
            after(dve.tensor_copy(startI[:, 0, :], start[:, :]))
            after(dve.tensor_scalar(startI[:, 1, :], start[:, :], float(P - 1), None, ALU.add))
            after(dve.tensor_scalar(startI[:, :, :], startI[:, :, :], 7, None, ALU.arith_shift_right))
            after(dve.tensor_copy(tiles[:, :, :], startI[:, :, :]))
            after(dve.tensor_tensor(many[:, :], tiles[:, 1, 1:NT + 1], tiles[:, 0, 0:NT], ALU.subtract))
            after(dve.tensor_tensor_scan(vend[:, :], many[:, :], zero[:, :], 0.0, ALU.add, ALU.add))
            after(dve.tensor_tensor(shift[:, :], many[:, :], vend[:, :], ALU.subtract))
            after(dve.tensor_tensor(shift[:, :], shift[:, :], tiles[:, 0, 0:NT], ALU.add))
            whole = [P, VB, NT]
            after(dve.tensor_tensor(mask[:, :, :], vend[:, :].unsqueeze(1).to_broadcast(whole),
                                    v[:, :].unsqueeze(2).to_broadcast(whole), ALU.is_le))
            after(dve.tensor_reduce(wv[:, :], mask[:, :, :], AX.X, ALU.add))
            after(dve.tensor_tensor(mask[:, :, :], K["iota"][:, 0:NT].unsqueeze(1).to_broadcast(whole),
                                    wv[:, :].unsqueeze(2).to_broadcast(whole), ALU.is_equal))
            after(dve.tensor_tensor(mask[:, :, :], mask[:, :, :], shift[:, :].unsqueeze(1).to_broadcast(whole), ALU.mult))
            after(dve.tensor_reduce(tv[:, :], mask[:, :, :], AX.X, ALU.add))
            after(dve.tensor_tensor(tv[:, :], tv[:, :], v[:, :], ALU.add))
            after(dve.tensor_scalar(wI[:, :], wv[:, :], float(NT - 1), None, ALU.min))
            after(dve.tensor_scalar(w0[:, :], wv[:, :], float(P), None, ALU.mult))
            for k in range(6):
                after(dve.tensor_scalar(tF[:, k, :], tv[:, :], float(ETILES - 1), float(k * ETILES), ALU.min, ALU.add))
            dve.tensor_copy(tI[:, :, :], tF[:, :, :]).then_inc(planned, 1)
            dve.wait_ge(fetched, 16 * 6 * VB)
            for b in range(VB):
                dve.tensor_scalar(vr[:, 1, b, :], vr[:, 1, b, :], w0[:, b:b + 1], None, ALU.subtract).then_inc(local, 1)


def aggregate(nc, K, zt):
    G, SLOTS = 4, 4
    IT = VISITS // (G * SLOTS)
    with ExitStack() as ctx:
        def sb(name, shape, dt=F32):
            return ctx.enter_context(nc.sbuf_tensor(name, shape, dt))

        def sem(name):
            return ctx.enter_context(nc.semaphore(name))

        acc = sb("acc", [P, NT, ZW])
        idx = sb("vidx", [P, SLOTS, G], I32)
        z = sb("z", [P, SLOTS, G, ZW])
        hot = sb("hot", [P, SLOTS, G, P])
        rden = sb("rden", [P, NT, HEADS])
        ups = [ctx.enter_context(nc.psum_tensor(f"ups{b}", [P, 512], F32)) for b in range(8)]
        idx_ready = sem("vidx_ready")
        landed = [sem(f"z_landed{s}") for s in range(SLOTS)]
        scaled = sem("scaled")
        summed = sem("summed")
        added = sem("added")
        begun = sem("visit_groups_begun")
        fin = sem("gnn_fin")
        block = ctx.enter_context(nc.Block())

        @block.gpsimd
        def _(pool):
            with pool.Fori(0, IT) as i:
                for s in range(SLOTS):
                    pool.wait_ge(idx_ready, i * SLOTS + s + 1)
                    pool.wait_ge(summed, i * SLOTS + s + 1)
                    pool.sem_inc(begun, 1)
                    for g in range(G):
                        pool.indirect_dma_start(
                            out=z[:, s, g, 0:D], out_offset=None, in_=zt[:, :],
                            in_offset=bass.IndirectOffsetOnAxis(ap=idx[:, s, g:g + 1], axis=0)).then_inc(landed[s], 16)

        @block.vector
        def _(dve):
            dve.memset(acc[:, :, :], 0.0).then_inc(fin, 1)
            dve.wait_ge(fin, 1)
            for s in range(SLOTS):
                dve.tensor_copy(idx[:, s, :], K["srcV"][:, s * G:(s + 1) * G]).then_inc(idx_ready, 1)

            def accumulate(i, s):
                first = (i * SLOTS + s) * G
                ws = [dve.value_load(K["wrow"][0:1, bass.ds(first + g, 1)], min_val=0, max_val=NT - 1) for g in range(G)]
                dve.wait_ge(summed, i * SLOTS + s + 1 + SLOTS)
                for g in range(G):
                    dve.wait_ge(added, (i * SLOTS + s) * G + g)
                    into = acc[:, bass.ds(ws[g], 1), :].rearrange("p a z -> p (a z)")
                    dve.tensor_tensor(into, ups[(s % 2) * G + g][:, 0:ZW], into, ALU.add).then_inc(added, 1)

            with dve.Fori(0, IT) as i:
                for s in range(SLOTS):
                    dve.wait_ge(landed[s], (i + 1) * (16 * G))
                    first = (i * SLOTS + s) * G
                    ex = K["exV"][:, bass.ds(first, G), :]
                    heads = z[:, s, :, 0:D].rearrange("p g (h f) -> p g h f", h=HEADS)
                    dve.tensor_tensor(heads, heads, ex.unsqueeze(3).to_broadcast([P, G, HEADS, FH]), ALU.mult).then_inc(scaled, 1)
                    dve.tensor_copy(z[:, s, :, D:ZW], ex).then_inc(scaled, 1)
                    dve.tensor_tensor(hot[:, s, :, :], K["iota"][:, :].unsqueeze(1).to_broadcast([P, G, P]),
                                      K["dstV"][:, bass.ds(first, G)].unsqueeze(2).to_broadcast([P, G, P]),
                                      ALU.is_equal).then_inc(scaled, 1)
                    dve.tensor_copy(idx[:, s, :], K["srcV"][:, bass.ds(first + SLOTS * G, G)]).then_inc(idx_ready, 1)
                    if s >= 1:
                        accumulate(i, s - 1)
                accumulate(i, SLOTS - 1)
            dve.wait_ge(added, VISITS)
            dve.tensor_scalar(rden[:, :, :], acc[:, :, D:ZW], 1e-30, None, ALU.max).then_inc(fin, 1)
            dve.wait_ge(fin, 2)
            dve.reciprocal(rden[:, :, :], rden[:, :, :]).then_inc(fin, 1)
            dve.wait_ge(fin, 3)
            for h in range(HEADS):
                part = acc[:, :, h * FH:(h + 1) * FH]
                dve.tensor_tensor(part, part, rden[:, :, h:h + 1].to_broadcast([P, NT, FH]), ALU.mult).then_inc(fin, 1)
            dve.wait_ge(fin, 7)
            dve.tensor_tensor(K["x2"][:, :, :], K["x2"][:, :, :], acc[:, :, 0:D], ALU.add)

        @block.tensor
        def _(pe):
            pe.sem_inc(summed, SLOTS)
            with pe.Fori(0, IT) as i:
                for s in range(SLOTS):
                    pe.wait_ge(scaled, 3 * (i * SLOTS + s + 1))
                    if s < 2:
                        pe.wait_ge(added, i * (SLOTS * G) + 0 if s == 0 else i * (SLOTS * G))
                    else:
                        pe.wait_ge(added, i * (SLOTS * G) + (s - 1) * G)
                    for g in range(G):
                        mm = pe.matmul(ups[(s % 2) * G + g][:, 0:ZW], hot[:, s, g, :], z[:, s, g, :],
                                       start=True, stop=True)
                    mm.then_inc(summed, 1)


def route(nc, K, Wr, br, xd):
    C = 7
    with ExitStack() as ctx:
        def sb(name, shape, dt=F32):
            return ctx.enter_context(nc.sbuf_tensor(name, shape, dt))

        def sem(name):
            return ctx.enter_context(nc.semaphore(name))

        X = K["x2"]
        wr = sb("wr", [P, KD, NE])
        brb = sb("brb", [P, NE])
        tri = sb("tri", [P, P])
        stats = sb("rstats", [P, C, 6])
        mv = sb("rmv", [P, C, 2])
        vinv = sb("rvinv", [P, C])
        rstd = sb("rrstd", [P, C])
        inner = sb("inner", [P, C])
        rin = sb("rin", [P, C])
        xt = sb("xt", [P, C, D])
        xT = sb("rxT", [P, C, D])
        lg = sb("lg", [P, NT, NE])
        tmp = sb("rtmp", [P, NT, NE])
        hot = [sb(f"chosen{k}", [P, NT, NE]) for k in range(2)]
        both = sb("both", [P, NT, NE])
        place = sb("place", [P, NT, NE])
        zero = sb("rzero", [P, NT])
        top = sb("top", [P, 2, NT])
        pick = sb("pick", [P, NT])
        p2 = sb("p2", [P, NT])
        total = sb("total", [P, NT, NE])
        upto = sb("upto", [P, NT, NE])
        ntile = sb("ntile", [P, NE])
        ntileI = sb("ntileI", [P, NE], I32)
        tend = sb("tend", [P, NE])
        base = sb("base", [P, NE])
        tmask = sb("tmask", [1, P, NE])
        trow = sb("trow", [1, P])
        tps = [ctx.enter_context(nc.psum_tensor(f"rtps{b}", [P, 512], F32)) for b in range(2)]
        lps = ctx.enter_context(nc.psum_tensor("lps", [P, 512], F32))
        cps = [ctx.enter_context(nc.psum_tensor(f"rcps{b}", [P, 512], F32)) for b in range(2)]
        par_in = sem("par_in")
        x2_out = sem("x2_out")
        tri_done = sem("tri_done")
        ln_step = sem("rln_step")
        root = sem("rroot")
        begun = sem("raggregation_begun")
        xt_ready = sem("xt_ready")
        turned = sem("rturned")
        xT_ready = sem("rxT_ready")
        lg_ready = sem("lg_ready")
        lg_out = sem("lg_out")
        step = sem("route_step")
        p2_done = sem("p2_done")
        counted = sem("rcounted")
        block = ctx.enter_context(nc.Block())
        L = 2 * C + 4

        @block.sync
        def _(sp):
            for c in range(NT // C):
                sp.dma_start(K["x2d"][c * C * P:(c + 1) * C * P, :].rearrange("(t p) d -> p t d", p=P),
                             X[:, c * C:(c + 1) * C, :]).then_inc(x2_out, 16)
            sp.dma_start(wr[:, :, :], Wr.rearrange("(k p) e -> p k e", p=P)).then_inc(par_in, 16)
            sp.dma_start(brb[:, :], br.partition_broadcast(P)).then_inc(par_in, 16)
            sp.wait_ge(x2_out, 16 * (NT // C))

        @block.gpsimd
        def _(pool):
            pool.affine_select(out=tri[:, :], in_=K["ones"][:, :], compare_op=ALU.is_gt, fill=0.0,
                               base=0, pattern=[[1, P]], channel_multiplier=-1).then_inc(tri_done, 1)

        @block.vector
        def _(dve):
            with dve.Fori(0, NT // C) as c:
                dve.wait_ge(xt_ready, c * C)
                for j in range(C):
                    dve.bn_stats(stats[:, j, :], X[:, c * C + j, :]).then_inc(ln_step, 1)
                dve.wait_ge(ln_step, c * L + C)
                dve.sem_inc(begun, 1)
                for j in range(C):
                    dve.bn_aggr(mv[:, j, :], stats[:, j, :]).then_inc(ln_step, 1)
                dve.wait_ge(ln_step, c * L + 2 * C)
                dve.tensor_scalar(vinv[:, :], mv[:, :, 1], EPS, None, ALU.add).then_inc(ln_step, 1)
                dve.wait_ge(ln_step, c * L + 2 * C + 1)
                dve.reciprocal(vinv[:, :], vinv[:, :]).then_inc(ln_step, 1)
                dve.wait_ge(ln_step, c * L + 2 * C + 2)
                dve.tensor_tensor(inner[:, :], mv[:, :, 1], vinv[:, :], ALU.mult).then_inc(ln_step, 1)
                dve.wait_ge(ln_step, c * L + 2 * C + 3)
                dve.tensor_scalar(inner[:, :], inner[:, :], EPS, None, ALU.add).then_inc(ln_step, 1)
                dve.wait_ge(ln_step, c * L + 2 * C + 4)
                dve.reciprocal(inner[:, :], inner[:, :]).then_inc(step, 1)
                dve.wait_ge(root, 2 * c + 2)
                dve.tensor_copy(K["mean"][:, bass.ds(c * C, C)], mv[:, :, 0]).then_inc(step, 1)
                dve.tensor_tensor(K["rstd"][:, bass.ds(c * C, C)], rstd[:, :], rin[:, :], ALU.mult).then_inc(step, 1)
                dve.wait_ge(step, c * 3 + 3)
                for j in range(C):
                    dve.wait_ge(turned, c * C + j + 1)
                    dve.tensor_scalar(xt[:, j, :], X[:, c * C + j, :], mv[:, j, 0:1], rstd[:, j:j + 1],
                                      ALU.subtract, ALU.mult).then_inc(xt_ready, 1)
            n = Tally()
            n.n = 3 * (NT // C)

            def after(ins):
                ins.then_inc(step, n.one())
                dve.wait_ge(step, n.n)

            whole = [P, NT, NE]
            number = K["iota"][:, 0:NE].unsqueeze(1).to_broadcast(whole)
            after(dve.memset(zero[:, :], 0.0))
            dve.wait_ge(lg_out, NT // C)
            dve.wait_ge(par_in, 32)
            after(dve.tensor_tensor(lg[:, :, :], lg[:, :, :], brb[:, :].unsqueeze(1).to_broadcast(whole), ALU.add))
            for k in range(2):
                after(dve.tensor_reduce(top[:, k, :], lg[:, :, :], AX.X, ALU.max))
                after(dve.tensor_tensor(tmp[:, :, :], lg[:, :, :], top[:, k, :].unsqueeze(2).to_broadcast(whole), ALU.not_equal))
                after(dve.scalar_tensor_tensor(out=tmp[:, :, :], in0=tmp[:, :, :], scalar=float(NE), in1=number,
                                               op0=ALU.mult, op1=ALU.add))
                after(dve.tensor_reduce(pick[:, :], tmp[:, :, :], AX.X, ALU.min))
                after(dve.tensor_tensor(hot[k][:, :, :], number, pick[:, :].unsqueeze(2).to_broadcast(whole), ALU.is_equal))
                if k == 0:
                    after(dve.scalar_tensor_tensor(out=lg[:, :, :], in0=hot[0][:, :, :], scalar=FAR, in1=lg[:, :, :],
                                                   op0=ALU.mult, op1=ALU.add))
            after(dve.tensor_tensor(both[:, :, :], hot[0][:, :, :], hot[1][:, :, :], ALU.add))
            dve.wait_ge(tri_done, 1)
            after(dve.tensor_scalar(both[:, NT - 1, :], both[:, NT - 1, :], tri[:, TAIL:TAIL + 1], None, ALU.mult))
            K["both_at"] = n.n
            after(dve.tensor_tensor(pick[:, :], top[:, 1, :], top[:, 0, :], ALU.subtract))
            K["pick_at"] = n.n
            dve.wait_ge(p2_done, 1)
            after(dve.tensor_scalar(K["gate"][:, 0, :], p2[:, :], 1.0, None, ALU.add))
            after(dve.reciprocal(K["gate"][:, 0, :], K["gate"][:, 0, :]))
            after(dve.tensor_tensor(K["gate"][:, 1, :], p2[:, :], K["gate"][:, 0, :], ALU.mult))
            dve.wait_ge(counted, 1)
            after(dve.tensor_copy(total[:, :, :], cps[1][:, 0:NT * NE].rearrange("p (t e) -> p t e", e=NE)))
            for e in range(NE):
                after(dve.tensor_tensor_scan(upto[:, :, e], total[:, :, e], zero[:, :], 0.0, ALU.add, ALU.add))
            after(dve.tensor_scalar(ntileI[:, :], upto[:, NT - 1, :], float(P - 1), None, ALU.add))
            after(dve.tensor_scalar(ntileI[:, :], ntileI[:, :], 7, None, ALU.arith_shift_right))
            after(dve.tensor_copy(ntile[:, :], ntileI[:, :]))
            after(dve.tensor_tensor_scan(tend[:, :], ntile[:, :], zero[:, 0:NE], 0.0, ALU.add, ALU.add))
            after(dve.tensor_tensor(base[:, :], tend[:, :], ntile[:, :], ALU.subtract))
            after(dve.tensor_scalar(base[:, :], base[:, :], float(P), None, ALU.mult))
            after(dve.tensor_tensor(place[:, :, :], upto[:, :, :], total[:, :, :], ALU.subtract))
            after(dve.tensor_tensor(place[:, :, :], place[:, :, :],
                                    cps[0][:, 0:NT * NE].rearrange("p (t e) -> p t e", e=NE), ALU.add))
            after(dve.tensor_tensor(place[:, :, :], place[:, :, :], base[:, :].unsqueeze(1).to_broadcast(whole), ALU.add))
            for k in range(2):
                after(dve.tensor_tensor(hot[k][:, :, :], hot[k][:, :, :], place[:, :, :], ALU.mult))
                after(dve.tensor_reduce(pick[:, :], hot[k][:, :, :], AX.X, ALU.add))
                after(dve.tensor_copy(K["slot"][:, k, 0:NT], pick[:, :]))
            tw = [1, P, NE]
            after(dve.tensor_tensor(tmask[:, :, :], tend[0:1, :].unsqueeze(1).to_broadcast(tw),
                                    K["iota"][0:1, :].unsqueeze(2).to_broadcast(tw), ALU.is_le))
            after(dve.tensor_reduce(trow[:, :], tmask[:, :, :], AX.X, ALU.add))
            after(dve.tensor_scalar(K["erow"][:, :], trow[:, :], float(NE - 1), None, ALU.min))

        @block.scalar
        def _(act):
            with act.Fori(0, NT // C) as c:
                act.wait_ge(ln_step, c * L + 2 * C + 2)
                act.activation(rstd[:, :], vinv[:, :], ACT.Sqrt).then_inc(root, 1)
                act.wait_ge(step, c * 3 + 1)
                act.activation(rin[:, :], inner[:, :], ACT.Sqrt).then_inc(root, 1)
                for j in range(C):
                    act.wait_ge(turned, c * C + j + 1 + C)
                    act.activation(xT[:, j, :], tps[j % 2][:, 0:D], ACT.Copy).then_inc(xT_ready, 1)
                act.wait_ge(lg_ready, c * C + C)
                act.activation(lg[:, bass.ds(c * C, C), :], lps[:, 0:C * NE].rearrange("p (t e) -> p t e", e=NE),
                               ACT.Copy).then_inc(lg_out, 1)
            act.wait_ge(step, K["pick_at"])
            act.activation(p2[:, :], pick[:, :], ACT.Exp).then_inc(p2_done, 1)

        @block.tensor
        def _(pe):
            pe.sem_inc(turned, C)
            pe.wait_ge(par_in, 32)
            with pe.Fori(0, NT // C) as c:
                for j in range(C):
                    pe.wait_ge(xt_ready, c * C + j + 1)
                    pe.wait_ge(xT_ready, c * C + j - 1 if j else c * C)
                    for k in range(KD):
                        mm = pe.transpose(tps[j % 2][:, k * P:(k + 1) * P], xt[:, j, k * P:(k + 1) * P],
                                          K["ident"][:, :])
                    mm.then_inc(turned, 1)
                pe.wait_ge(lg_out, c * 1)
                for j in range(C):
                    pe.wait_ge(xT_ready, c * C + j + 1)
                    for k in range(KD):
                        mm = pe.matmul(lps[:, j * NE:(j + 1) * NE], xT[:, j, k * P:(k + 1) * P], wr[:, k, :],
                                       start=(k == 0), stop=(k == KD - 1))
                    mm.then_inc(lg_ready, 1)
            pe.wait_ge(tri_done, 1)
            pe.wait_ge(step, K["both_at"])
            flat = both[:, :, :].rearrange("p t e -> p (t e)")
            pe.matmul(cps[0][:, 0:NT * NE], tri[:, :], flat, start=True, stop=True)
            pe.matmul(cps[1][:, 0:NT * NE], K["ones"][:, :], flat, start=True, stop=True).then_inc(counted, 1)


def dispatch(nc, K, xd):
    C = 7
    with ExitStack() as ctx:
        def sb(name, shape, dt=F32):
            return ctx.enter_context(nc.sbuf_tensor(name, shape, dt))

        def sem(name):
            return ctx.enter_context(nc.semaphore(name))

        xn = sb("dxn", [P, C, D])
        parts = sb("parts", [P, C, 2 * D], F16)
        idx = sb("didx", [P, C, 2], I32)
        normed = sem("normed")
        split = sem("split")
        sent = [sem(f"sent{j}") for j in range(C)]
        begun = sem("dispatch_begun")
        block = ctx.enter_context(nc.Block())

        def send(pool, j, rows):
            for k in range(2):
                pool.indirect_dma_start(
                    out=xd[:, :], out_offset=bass.IndirectOffsetOnAxis(ap=idx[0:rows, j, k:k + 1], axis=0),
                    in_=parts[0:rows, j, :], in_offset=None).then_inc(sent[j], 16)

        @block.vector
        def _(dve):
            with dve.Fori(0, NT // C) as c:
                for j in range(C):
                    t = c * C + j
                    dve.tensor_scalar(xn[:, j, :], K["x2"][:, t, :], K["mean"][:, bass.ds(t, 1)], K["rstd"][:, bass.ds(t, 1)],
                                      ALU.subtract, ALU.mult).then_inc(normed, 1)
                for j in range(C):
                    t = c * C + j
                    dve.wait_ge(sent[j], 32 * c)
                    dve.tensor_copy(idx[:, j, :], K["slot"][:, :, bass.ds(t, 1)].rearrange("p k a -> p (k a)")).then_inc(split, 1)
                    dve.wait_ge(normed, t + 1)
                    dve.tensor_copy(parts[:, j, 0:D], xn[:, j, :]).then_inc(split, 1)
                    dve.wait_ge(split, 3 * t + 2)
                    dve.tensor_tensor(parts[:, j, D:2 * D], xn[:, j, :], parts[:, j, 0:D], ALU.subtract).then_inc(split, 1)
                dve.wait_ge(split, 3 * C * (c + 1))

        @block.gpsimd
        def _(pool):
            with pool.Fori(0, NT // C - 1) as c:
                for j in range(C):
                    pool.wait_ge(split, 3 * (c * C + j + 1))
                    pool.sem_inc(begun, 1)
                    send(pool, j, P)
            for j in range(C):
                pool.wait_ge(split, 3 * (NT - C + j + 1))
                send(pool, j, P if j < C - 1 else TAIL)
            for j in range(C):
                pool.wait_ge(sent[j], 32 * (NT // C))


def prepare_weights(nc, K, ln_g, ln_b, W1, b1, W2, b2):
    with ExitStack() as ctx:
        def sb(name, shape, dt=F32):
            return ctx.enter_context(nc.sbuf_tensor(name, shape, dt))

        def sem(name):
            return ctx.enter_context(nc.semaphore(name))

        stage = sb("stage", [P, 2, KD * HID])
        rowsb1 = sb("rowsb1", [NE * MH, P])
        rowsln = sb("rowsln", [2 * NE * KD, P])
        lnT = sb("lnT", [P, 2, NE, KD])
        gain = sb("gain", [P, NE, KD])
        b1T = sb("b1T", [P, NE, MH])
        tps = ctx.enter_context(nc.psum_tensor("wtps", [P, 512], F32))
        bps = [ctx.enter_context(nc.psum_tensor(f"bps{s}", [P, 512], F32)) for s in range(2)]
        small_in = sem("small_in")
        raw_in = [sem(f"raw_in{s}") for s in range(2)]
        small = sem("small")
        turned = sem("wturned")
        hi = sem("hi")
        lo = sem("lo")
        biased = sem("biased")
        bias_out = sem("bias_out")
        block = ctx.enter_context(nc.Block())

        @block.sync
        def _(sp):
            sp.dma_start(rowsb1[:, :], b1.rearrange("e (m p) -> (e m) p", p=P)).then_inc(small_in, 16)
            sp.dma_start(rowsln[0:NE * KD, :], ln_g.rearrange("e (k p) -> (e k) p", p=P)).then_inc(small_in, 16)
            sp.dma_start(rowsln[NE * KD:2 * NE * KD, :], ln_b.rearrange("e (k p) -> (e k) p", p=P)).then_inc(small_in, 16)
            sp.dma_start(K["b2b"][:, :, :], b2.partition_broadcast(P)).then_inc(small_in, 16)
            with sp.Fori(0, NE) as e:
                sp.wait_ge(lo, 3 * e)
                sp.dma_start(stage[:, 0, :].rearrange("p (k h) -> p k h", k=KD),
                             W1[bass.ds(e, 1), :, :].rearrange("a (k p) h -> p (a k) h", p=P)).then_inc(raw_in[0], 16)
                sp.dma_start(stage[:, 1, :].rearrange("p (m d) -> p m d", m=MH),
                             W2[bass.ds(e, 1), :, :].rearrange("a (m p) d -> p (a m) d", p=P)).then_inc(raw_in[1], 16)
            sp.wait_ge(small_in, 64)

        @block.tensor
        def _(pe):
            pe.wait_ge(small_in, 64)
            pe.transpose(tps[:, 0:NE * MH], rowsb1[:, :], K["ident"][0:NE * MH, 0:NE * MH])
            pe.transpose(tps[:, 64:64 + 2 * NE * KD], rowsln[:, :], K["ident"][0:2 * NE * KD, 0:2 * NE * KD]).then_inc(turned, 1)
            pe.wait_ge(small, 2)
            with pe.Fori(0, NE) as e:
                pe.wait_ge(raw_in[0], 16 * e + 16)
                pe.wait_ge(bias_out, e * 1)
                for m in range(MH):
                    for k in range(KD):
                        mm = pe.matmul(bps[0][:, m:m + 1], stage[:, 0, k * HID + m * P:k * HID + (m + 1) * P],
                                       K["lnb"][:, k, bass.ds(e, 1)], start=(k == 0), stop=(k == KD - 1))
                mm.then_inc(biased, 1)

        @block.scalar
        def _(act):
            act.wait_ge(small, 3)
            with act.Fori(0, NE) as e:
                act.wait_ge(raw_in[0], 16 * e + 16)
                for k in range(KD):
                    act.activation(K["w1"][:, 0, bass.ds(e, 1), k, :].rearrange("p a h -> p (a h)"),
                                   stage[:, 0, k * HID:(k + 1) * HID], ACT.Copy,
                                   scale=K["gain"][:, k, bass.ds(e, 1)]).then_inc(hi, 1)
                act.wait_ge(raw_in[1], 16 * e + 16)
                act.activation(K["w2"][:, 0, bass.ds(e, 1), :, :].rearrange("p a m d -> p (a m d)"),
                               stage[:, 1, :], ACT.Copy, scale=SC).then_inc(hi, 1)

        @block.vector
        def _(dve):
            dve.wait_ge(turned, 1)
            dve.tensor_copy(b1T[:, :, :], tps[:, 0:NE * MH].rearrange("p (e m) -> p e m", m=MH)).then_inc(small, 1)
            dve.tensor_copy(K["lnb"][:, :, :], tps[:, 64 + NE * KD:64 + 2 * NE * KD].rearrange("p (e k) -> p k e", k=KD)).then_inc(small, 1)
            dve.tensor_scalar(K["gain"][:, :, :], tps[:, 64:64 + NE * KD].rearrange("p (e k) -> p k e", k=KD),
                              SC, None, ALU.mult).then_inc(small, 1)
            dve.wait_ge(small, 3)
            with dve.Fori(0, NE) as e:
                for k in range(KD):
                    dve.wait_ge(hi, 3 * e + k + 1)
                    dve.scalar_tensor_tensor(out=K["w1"][:, 1, bass.ds(e, 1), k, :].rearrange("p a h -> p (a h)"),
                                             in0=stage[:, 0, k * HID:(k + 1) * HID], scalar=K["gain"][:, k, bass.ds(e, 1)],
                                             in1=K["w1"][:, 0, bass.ds(e, 1), k, :].rearrange("p a h -> p (a h)"),
                                             op0=ALU.mult, op1=ALU.subtract).then_inc(lo, 1)
                dve.wait_ge(biased, e + 1)
                dve.tensor_tensor(K["b1p"][:, bass.ds(e, 1), :].rearrange("p a m -> p (a m)"), bps[0][:, 0:MH],
                                  b1T[:, bass.ds(e, 1), :].rearrange("p a m -> p (a m)"), ALU.add).then_inc(bias_out, 1)
                dve.wait_ge(hi, 3 * e + 3)
                dve.scalar_tensor_tensor(out=K["w2"][:, 1, bass.ds(e, 1), :, :].rearrange("p a m d -> p (a m d)"),
                                         in0=stage[:, 1, :], scalar=SC,
                                         in1=K["w2"][:, 0, bass.ds(e, 1), :, :].rearrange("p a m d -> p (a m d)"),
                                         op0=ALU.mult, op1=ALU.subtract).then_inc(lo, 1)


def experts(nc, K, xd, yd):
    R = 3
    IT = ETL // R
    with ExitStack() as ctx:
        def sb(name, shape, dt=F32):
            return ctx.enter_context(nc.sbuf_tensor(name, shape, dt))

        def sem(name):
            return ctx.enter_context(nc.semaphore(name))

        ident16 = sb("ident16", [P, P], F16)
        xs = sb("xs", [P, R, 2 * D], F16)
        xT = sb("exT", [P, R, 2, KD, P], F16)
        h = sb("h", [P, 1, MH, P])
        hp = sb("hparts", [P, 2, 2, MH, P], F16)
        y = sb("y", [P, R, D])
        tps = [ctx.enter_context(nc.psum_tensor(f"etps{b}", [P, 1024], F16)) for b in range(2)]
        hps = [ctx.enter_context(nc.psum_tensor(f"hps{b}", [P, 512], F32)) for b in range(4)]
        yps = [ctx.enter_context(nc.psum_tensor(f"yps{b}", [P, 512], F32)) for b in range(2)]
        ident_ready = sem("ident_ready")
        x_in = [sem(f"slots_in{s}") for s in range(R)]
        turned = sem("eturned")
        xT_ready = sem("exT_ready")
        h_ready = sem("h_ready")
        acted = sem("acted")
        h_split = sem("h_split")
        y_ready = sem("y_ready")
        y_out = sem("y_out")
        y_stored = [sem(f"y_stored{s}") for s in range(R)]
        block = ctx.enter_context(nc.Block())

        @block.sync
        def _(sp):
            def load(n, s):
                sp.dma_start(xs[:, s, :], xd[bass.ds(n * P, P), :]).then_inc(x_in[s], 16)

            load(0, 0)
            load(1, 1)
            with sp.Fori(0, IT) as i:
                for s in range(R):
                    n = i * R + s
                    sp.wait_ge(turned, n)
                    load(n + 2, (s + 2) % R)
                    sp.wait_ge(y_out, n + 1)
                    sp.dma_start(yd[bass.ds(n * P, P), :], y[:, s, :]).then_inc(y_stored[s], 16)
            for s in range(R):
                sp.wait_ge(y_stored[s], 16 * IT)
                sp.wait_ge(x_in[s], 16 * (IT + (1 if s < 2 else 0)))

        @block.tensor
        def _(pe):
            def first(n, s, e):
                b = s % 2
                for part in range(2):
                    for k in range(KD):
                        at = part * D + k * P
                        mm = pe.transpose(tps[b][:, (part * KD + k) * P:(part * KD + k + 1) * P], xs[:, s % R, at:at + P],
                                          ident16[:, :])
                mm.then_inc(turned, 1)
                return b

            def layer1(n, s, e, b):
                for m in range(MH):
                    out = hps[2 * b + m // 4][:, (m % 4) * P:(m % 4 + 1) * P]
                    terms = [(wp, xp, k) for wp, xp in ((0, 0), (0, 1), (1, 0)) for k in range(KD)]
                    for q, (wp, xp, k) in enumerate(terms):
                        mm = pe.matmul(out, K["w1"][:, wp, bass.ds(e, 1), k, m * P:(m + 1) * P].rearrange("p a h -> p (a h)"),
                                       xT[:, s % R, xp, k, :], start=(q == 0), stop=(q == len(terms) - 1))
                    if m % 4 == 3:
                        mm.then_inc(h_ready, 1)

            def layer2(s, e):
                b = s % 2
                terms = [(m, hpart, wp) for m in range(MH) for hpart, wp in ((0, 0), (0, 1), (1, 0))]
                for q, (m, hpart, wp) in enumerate(terms):
                    mm = pe.matmul(yps[b][:, 0:D], hp[:, hpart, s % 2, m, :],
                                   K["w2"][:, wp, bass.ds(e, 1), m, :].rearrange("p a d -> p (a d)"),
                                   start=(q == 0), stop=(q == len(terms) - 1))
                mm.then_inc(y_ready, 1)

            def expert_of(n):
                return pe.value_load(K["erow"][0:1, bass.ds(n, 1)], min_val=0, max_val=NE - 1)

            pe.wait_ge(ident_ready, 1)
            pe.wait_ge(x_in[0], 16)
            first(0, 0, None)
            pe.wait_ge(xT_ready, 1)
            layer1(0, 0, expert_of(0), 0)
            with pe.Fori(0, ETL // (2 * R)) as i:
                for s in range(2 * R):
                    n = i * (2 * R) + s
                    e_now, e_next = expert_of(n), expert_of(n + 1)
                    pe.wait_ge(x_in[(s + 1) % R], 32 * i + 16 * ((s + 1) // R) + 16)
                    pe.wait_ge(xT_ready, n + 0)
                    b = first(n + 1, s + 1, None)
                    pe.wait_ge(xT_ready, n + 2)
                    pe.wait_ge(acted, n * MH)
                    layer1(n + 1, s + 1, e_next, b)
                    pe.wait_ge(h_split, 2 * n + 2)
                    if s >= 2:
                        pe.wait_ge(y_out, n - 1)
                    else:
                        pe.wait_ge(y_out, i * (2 * R))
                    layer2(s, e_now)

        @block.scalar
        def _(act):
            with act.Fori(0, ETL // (2 * R)) as i:
                for s in range(2 * R):
                    n = i * (2 * R) + s
                    e = act.value_load(K["erow"][0:1, bass.ds(n, 1)], min_val=0, max_val=NE - 1)
                    act.wait_ge(turned, n + 1)
                    act.activation(xT[:, s % R, :, :, :].rearrange("p a k n -> p (a k n)"), tps[s % 2][:, 0:2 * D],
                                   ACT.Copy).then_inc(xT_ready, 1)
                    act.wait_ge(h_split, 2 * n)
                    for m in range(MH):
                        if m % 4 == 0:
                            act.wait_ge(h_ready, 2 * n + m // 4 + 1)
                        act.activation(h[:, 0, m, :], hps[2 * (s % 2) + m // 4][:, (m % 4) * P:(m % 4 + 1) * P], ACT.Gelu,
                                       bias=K["b1p"][:, bass.ds(e, 1), m], scale=1.0 / SC).then_inc(acted, 1)
            act.wait_ge(turned, ETL + 1)
            act.activation(xT[:, 0, :, :, :].rearrange("p a k n -> p (a k n)"), tps[0][:, 0:2 * D], ACT.Copy).then_inc(xT_ready, 1)

        @block.vector
        def _(dve):
            dve.tensor_copy(ident16[:, :], K["ident"][:, :]).then_inc(ident_ready, 1)
            with dve.Fori(0, ETL // (2 * R)) as i:
                for s in range(2 * R):
                    n = i * (2 * R) + s
                    r = s % R
                    e = dve.value_load(K["erow"][0:1, bass.ds(n, 1)], min_val=0, max_val=NE - 1)
                    dve.wait_ge(acted, (n + 1) * MH)
                    dve.tensor_copy(hp[:, 0, s % 2, :, :], h[:, 0, :, :]).then_inc(h_split, 1)
                    dve.wait_ge(h_split, 2 * n + 1)
                    dve.tensor_tensor(hp[:, 1, s % 2, :, :], h[:, 0, :, :], hp[:, 0, s % 2, :, :], ALU.subtract).then_inc(h_split, 1)
                    if s >= R:
                        dve.wait_ge(y_stored[r], 32 * i + 16)
                    else:
                        dve.wait_ge(y_stored[r], 32 * i)
                    dve.wait_ge(y_ready, n + 1)
                    dve.scalar_tensor_tensor(out=y[:, r, :], in0=yps[s % 2][:, 0:D], scalar=1.0 / SC,
                                             in1=K["b2b"][:, bass.ds(e, 1), :].rearrange("p a d -> p (a d)"),
                                             op0=ALU.mult, op1=ALU.add).then_inc(y_out, 1)


def combine(nc, K, yd, out):
    C = 7
    with ExitStack() as ctx:
        def sb(name, shape, dt=F32):
            return ctx.enter_context(nc.sbuf_tensor(name, shape, dt))

        def sem(name):
            return ctx.enter_context(nc.semaphore(name))

        idx = sb("cidx", [P, 2, C], I32)
        yy = sb("yy", [P, C, 2, D])
        xo = sb("xo", [P, 2 * C, D])
        idx_ready = sem("cidx_ready")
        landed = [sem(f"y_landed{j}") for j in range(C)]
        mixed = sem("mixed")
        x2_in = [sem(f"x2_in{s}") for s in range(2)]
        stored = [sem(f"out_stored{s}") for s in range(2)]
        begun = sem("combine_begun")
        block = ctx.enter_context(nc.Block())

        @block.gpsimd
        def _(pool):
            with pool.Fori(0, NT // C) as c:
                for j in range(C):
                    pool.wait_ge(idx_ready, c * C + j + 1)
                    pool.sem_inc(begun, 1)
                    for k in range(2):
                        pool.indirect_dma_start(
                            out=yy[:, j, k, :], out_offset=None, in_=yd[:, :],
                            in_offset=bass.IndirectOffsetOnAxis(ap=idx[:, k, j:j + 1], axis=0)).then_inc(landed[j], 16)

        @block.vector
        def _(dve):
            for j in range(C):
                dve.tensor_copy(idx[:, :, j], K["slot"][:, :, j]).then_inc(idx_ready, 1)

            def mix(c, half):
                dve.wait_ge(x2_in[half], (c // 2) * 16 + 16 if isinstance(c, int) else c * 8 + 16 - 8 * half)
                for j in range(C):
                    t = c * C + j
                    tile = xo[:, half * C + j, :]
                    dve.wait_ge(landed[j], 32 * c + 32)
                    for k in range(2):
                        dve.scalar_tensor_tensor(out=tile, in0=yy[:, j, k, :], scalar=K["gate"][:, k, bass.ds(t, 1)], in1=tile,
                                                 op0=ALU.mult, op1=ALU.add).then_inc(mixed, 1)
                        dve.wait_ge(mixed, 2 * t + k + 1)
                    dve.tensor_copy(idx[:, :, j], K["slot"][:, :, bass.ds(t + C, 1)].rearrange("p k a -> p (k a)")).then_inc(idx_ready, 1)

            with dve.Fori(0, NT // C - 1, 2) as c:
                mix(c, 0)
                mix(c + 1, 1)
            mix(NT // C - 1, 0)

        @block.sync
        def _(sp):
            def rows(dram, c):
                return dram[bass.ds(c * (C * P), C * P), :].rearrange("(t p) d -> p t d", p=P)

            def load(c, half):
                sp.dma_start(xo[:, half * C:(half + 1) * C, :], rows(K["x2d"], c)).then_inc(x2_in[half], 16)

            load(0, 0)
            load(1, 1)
            for c in range(NT // C - 1):
                sp.wait_ge(mixed, 2 * C * c + 2 * C)
                sp.dma_start(rows(out, c), xo[:, (c % 2) * C:(c % 2 + 1) * C, :]).then_inc(stored[c % 2], 16)
                if c + 2 < NT // C:
                    sp.wait_ge(stored[c % 2], 16 * (c // 2 + 1))
                    load(c + 2, c % 2)
            sp.wait_ge(mixed, 2 * NT)
            sp.dma_start(out[(NT - C) * P:(NT - 1) * P, :].rearrange("(t p) d -> p t d", p=P),
                         xo[:, 0:C - 1, :]).then_inc(stored[0], 16)
            sp.dma_start(out[(NT - 1) * P:NODES, :], xo[0:TAIL, C - 1, :]).then_inc(stored[0], 16)
            sp.wait_ge(stored[0], 16 * 5)
            sp.wait_ge(stored[1], 16 * 3)


def clear_slots(nc, K, xd):
    with ExitStack() as ctx:
        zeros = ctx.enter_context(nc.sbuf_tensor("zeros", [P, 2 * D], F16))
        zeroed = ctx.enter_context(nc.semaphore("slots_zeroed"))
        cleared = ctx.enter_context(nc.semaphore("slots_cleared"))
        block = ctx.enter_context(nc.Block())

        @block.vector
        def _(dve):
            dve.memset(zeros[:, :], 0.0).then_inc(zeroed, 1)

        @block.sync
        def _(sp):
            sp.wait_ge(zeroed, 1)
            with sp.Fori(0, ETL + 2) as t:
                sp.dma_start(xd[bass.ds(t * P, P), :], zeros[:, :]).then_inc(cleared, 16)
            sp.wait_ge(cleared, 16 * (ETL + 2))





def build(nc, x, src, dst, gnn_W, gnn_att, Wr, br, ln_g, ln_b, W1, b1, W2, b2, out):
    def scratch(name, shape, dt=F32):
        return nc.dram_tensor(name, shape, dt).ap()

    zt = scratch("zt", [NT * P, D])
    es_tab = scratch("es_tab", [NT * P, HEADS])
    ed_tab = scratch("ed_tab", [NT * P, HEADS])
    rec = scratch("rec", [6, P * EC])
    wtab = scratch("wtab", [VB * P], I32)
    xd = scratch("xd", [(ETL + 2) * P, 2 * D], F16)
    yd = scratch("yd", [ETL * P, D])
    with ExitStack() as ctx:
        def sb(name, shape, dt=F32):
            return ctx.enter_context(nc.sbuf_tensor(name, shape, dt))

        K = {"ident": sb("ident", [P, P]), "ones": sb("ones", [P, P]), "iota": sb("iota", [P, P]),
             "mean": sb("mean", [P, NT]), "rstd": sb("rstd2", [P, NT]), "gate": sb("gate", [P, 2, NT]),
             "slot": sb("slot", [P, 2, NT + 7], I32), "erow": sb("erow", [1, P], I32),
             "x2d": scratch("x2d", [NT * P, D]), "ends_at": {}, "carried_at": {}}
        constants(nc, K)
        clear_slots(nc, K, xd)
        with ExitStack() as nodes:
            K["x2"] = nodes.enter_context(nc.sbuf_tensor("x2", [P, NT, D], F32))
            project_nodes(nc, K, x, gnn_W, gnn_att, zt, es_tab, ed_tab)
            with ExitStack() as gnn:
                K["counts"] = gnn.enter_context(nc.sbuf_tensor("counts", [P, NT + 1], F32))
                edge_scores(nc, K, src, dst, es_tab, ed_tab, rec)
                for name, shape, dt in (("srcV", [P, VB * P], I32), ("dstV", [P, VB * P], F32),
                                        ("exV", [P, VB * P, HEADS], F32), ("wrow", [1, VB * P], I32)):
                    K[name] = gnn.enter_context(nc.sbuf_tensor(name, shape, dt))
                plan_visits(nc, K, rec, wtab)
                aggregate(nc, K, zt)
            route(nc, K, Wr, br, xd)
            dispatch(nc, K, xd)
        with ExitStack() as ffn:
            for name, shape, dt in (("w1", [P, 2, NE, KD, HID], F16), ("w2", [P, 2, NE, MH, D], F16), ("b1p", [P, NE, MH], F32),
                                    ("b2b", [P, NE, D], F32), ("gain", [P, KD, NE], F32), ("lnb", [P, KD, NE], F32)):
                K[name] = ffn.enter_context(nc.sbuf_tensor(name + "_keep", shape, dt))
            prepare_weights(nc, K, ln_g, ln_b, W1, b1, W2, b2)
            experts(nc, K, xd, yd)
        combine(nc, K, yd, out)


_INS = ["x", "src", "dst", "L0_gnn_W", "L0_gnn_att", "L0_ffn_Wr", "L0_ffn_br", "L0_ffn_ln_g", "L0_ffn_ln_b",
        "L0_ffn_W1", "L0_ffn_b1", "L0_ffn_W2", "L0_ffn_b2"]


def kernel(**inputs):
    import numpy as _np
    import concourse.bacc as _bacc
    from concourse import mybir as _mybir
    from concourse.bass_utils import run_bass_kernel_spmd as _run

    nc = _bacc.Bacc("TRN2", target_bir_lowering=False, num_devices=1)
    arrays, args = {}, []
    for name in _INS:
        a = _np.ascontiguousarray(inputs[name])
        arrays[f"in_{name}_dram"] = a
        args.append(nc.dram_tensor(f"in_{name}_dram", a.shape, _mybir.dt.from_np(a.dtype), kind="ExternalInput").ap())
    args.append(nc.dram_tensor("out_0_dram", (NODES, D), _mybir.dt.float32, kind="ExternalOutput").ap())
    build(nc, *args)
    r = _run(nc, [arrays], core_ids=[0])
    return r.results[0]["out_0_dram"]
```

```python
from contextlib import ExitStack

import concourse.bass as bass
from concourse import mybir
from concourse.alu_op_type import AluOpType as ALU

ACT = mybir.ActivationFunctionType
F32 = mybir.dt.float32
F16 = mybir.dt.float16
BF16 = mybir.dt.bfloat16
I32 = mybir.dt.int32
AX = mybir.AxisListType

P = 128
D = 256
KD = D // P
HEADS = 4
FH = D // HEADS
ZW = D + HEADS
NODES = 6250
NT = -(-NODES // P)
TAIL = NODES - (NT - 1) * P
EDGES = 100000
EC = 784
FULLP = EDGES // EC
ETAIL = EDGES - FULLP * EC
ETILES = EC
VISITS = -(-(-(-EDGES // P) + 2 * NT) // 16) * 16
VB = -(-(VISITS + 16) // P)
FAR = -1.0e30
NEG = -1000.0
SLOPE = 0.01
EPS = 1e-5
NE = 8
HID = 1024
MH = HID // P
EP = 2 * P
ETL = (2 * NODES + NE * (EP - 1)) // EP
XTL = ETL + 4
SC = 64.0


class Tally:

    def __init__(self):
        self.n = 0

    def one(self):
        self.n += 1
        return 1


def constants(nc, K):
    with ExitStack() as ctx:
        ramp = ctx.enter_context(nc.sbuf_tensor("ramp", [P, P], I32))
        zeroed = ctx.enter_context(nc.semaphore("zeroed"))
        ramped = ctx.enter_context(nc.semaphore("ramped"))
        block = ctx.enter_context(nc.Block())

        @block.gpsimd
        def _(pool):
            pool.memset(K["ident"][:, :], 0.0).then_inc(zeroed, 1)
            pool.memset(K["ones"][:, :], 1.0)
            pool.memset(K["slot"][:, :, :], 0)
            pool.iota(ramp[:, :], pattern=[[1, P]], base=0, channel_multiplier=0).then_inc(ramped, 1)
            pool.wait_ge(zeroed, 1)
            pool.affine_select(out=K["ident"][:, :], in_=K["ident"][:, :], compare_op=ALU.not_equal,
                               fill=1.0, base=0, pattern=[[-1, P]], channel_multiplier=1)

        @block.vector
        def _(dve):
            dve.wait_ge(ramped, 1)
            dve.tensor_copy(K["iota"][:, :], ramp[:, :])


def project_nodes(nc, K, x, W, att, zt, es_tab, ed_edge):
    C = 7
    with ExitStack() as ctx:
        def sb(name, shape, dt=F32):
            return ctx.enter_context(nc.sbuf_tensor(name, shape, dt))

        def sem(name):
            return ctx.enter_context(nc.semaphore(name))

        X = K["x2"]
        wz = sb("wz", [P, KD, D + 2 * HEADS])
        attb = sb("attb", [P, HEADS, 2 * FH])
        watt = sb("watt", [P, KD, HEADS, 2, FH])
        stats = sb("stats", [P, C, 6])
        mv = sb("mv", [P, C, 2])
        vinv = sb("vinv", [P, C])
        rstd = sb("rstd", [P, C])
        xn = sb("xn", [P, C, D])
        xT = sb("xT", [P, C, D])
        zsb = sb("zsb", [P, C, D + 2 * HEADS])
        clear = sb("clear", [P, EC * HEADS])
        tps = [ctx.enter_context(nc.psum_tensor(f"tps{b}", [P, 512], F32)) for b in range(2)]
        zps = [ctx.enter_context(nc.psum_tensor(f"zps{b}", [P, 512], F32)) for b in range(2)]
        x_cleared = sem("x_cleared")
        x_in = sem("x_in")
        w_in = sem("w_in")
        wz_done = sem("wz_done")
        ln_step = sem("ln_step")
        root = sem("root")
        begun = sem("aggregation_begun")
        xn_ready = sem("xn_ready")
        turned = sem("turned")
        xT_ready = sem("xT_ready")
        z_ready = sem("z_ready")
        z_out = sem("z_out")
        z_stored = sem("z_stored")
        zsb_free = sem("zsb_free")
        att_kept = sem("att_kept")
        clear_ready = sem("clear_ready")
        cleared = sem("ed_edge_cleared")
        block = ctx.enter_context(nc.Block())

        @block.sync
        def _(sp):
            for k in range(KD):
                sp.dma_start(wz[:, k, 0:D].rearrange("p (h f) -> p h f", h=HEADS),
                             W[:, k * P:(k + 1) * P, :].rearrange("h p f -> p h f")).then_inc(w_in, 16)
            sp.dma_start(attb[:, :, :], att.partition_broadcast(P)).then_inc(w_in, 16)
            for c in range(6):
                sp.dma_start(X[:, 8 * c:8 * c + 8, :],
                             x[8 * c * P:8 * (c + 1) * P, :].rearrange("(t p) d -> p t d", p=P)).then_inc(x_in, 16)
            sp.wait_ge(x_cleared, 1)
            sp.dma_start(X[0:TAIL, NT - 1, :], x[(NT - 1) * P:NODES, :]).then_inc(x_in, 16)
            sp.wait_ge(clear_ready, 1)
            sp.dma_start(ed_edge[0:P * EC, :].rearrange("(p t) h -> p (t h)", p=P), clear[:, :]).then_inc(cleared, 16)
            sp.sem_inc(zsb_free, 1)
            with sp.Fori(0, NT // C) as c:
                sp.wait_ge(z_out, c * C + C + 2)
                sp.dma_start(zt[bass.ds(c * (C * P), C * P), :].rearrange("(t p) d -> p t d", p=P),
                             zsb[:, :, 0:D]).then_inc(z_stored, 16)
                sp.dma_start(es_tab[bass.ds(c * (C * P), C * P), :].rearrange("(t p) d -> p t d", p=P),
                             zsb[:, :, D:D + HEADS]).then_inc(z_stored, 16)
                sp.wait_ge(z_stored, c * 32 + 32)
                sp.sem_inc(zsb_free, 1)
            sp.wait_ge(cleared, 16)

        @block.gpsimd
        def _(pool):
            pool.memset(clear[:, :], 0.0).then_inc(clear_ready, 1)
            pool.sem_inc(att_kept, 1)
            with pool.Fori(0, NT // C) as c:
                pool.wait_ge(z_out, c * C + C + 2)
                pool.tensor_copy(K["att_node"][:, bass.ds(c * C, C), :], zsb[:, :, D:D + 2 * HEADS]).then_inc(att_kept, 1)

        @block.vector
        def _(dve):
            dve.sem_inc(xn_ready, 1)
            dve.memset(X[:, NT - 1, :], 0.0).then_inc(x_cleared, 1)
            dve.wait_ge(w_in, 16 * (KD + 1))
            for k in range(KD):
                for side in range(2):
                    dve.tensor_tensor(watt[:, k, :, side, :],
                                      wz[:, k, 0:D].rearrange("p (h f) -> p h f", h=HEADS),
                                      attb[:, :, side * FH:(side + 1) * FH], ALU.mult).then_inc(wz_done, 1)
            dve.wait_ge(wz_done, 4)
            for k in range(KD):
                for side in range(2):
                    dve.tensor_reduce(wz[:, k, D + side * HEADS:D + (side + 1) * HEADS],
                                      watt[:, k, :, side, :], AX.X, ALU.add).then_inc(wz_done, 1)
            dve.wait_ge(x_in, 16 * 7)
            with dve.Fori(0, NT // C) as c:
                dve.wait_ge(xn_ready, c * C + 1)
                for j in range(C):
                    dve.bn_stats(stats[:, j, :], X[:, c * C + j, :]).then_inc(ln_step, 1)
                dve.wait_ge(ln_step, c * (2 * C + 2) + C)
                dve.sem_inc(begun, 1)
                for j in range(C):
                    dve.bn_aggr(mv[:, j, :], stats[:, j, :]).then_inc(ln_step, 1)
                dve.wait_ge(ln_step, c * (2 * C + 2) + 2 * C)
                dve.tensor_scalar(vinv[:, :], mv[:, :, 1], EPS, None, ALU.add).then_inc(ln_step, 1)
                dve.wait_ge(ln_step, c * (2 * C + 2) + 2 * C + 1)
                dve.reciprocal(vinv[:, :], vinv[:, :]).then_inc(ln_step, 1)
                dve.wait_ge(root, c + 1)
                for j in range(C):
                    dve.wait_ge(turned, c * C + j + 1)
                    dve.tensor_scalar(xn[:, j, :], X[:, c * C + j, :], mv[:, j, 0:1], rstd[:, j:j + 1],
                                      ALU.subtract, ALU.mult).then_inc(xn_ready, 1)

        @block.scalar
        def _(act):
            act.sem_inc(xT_ready, 2)
            act.sem_inc(z_out, 2)
            with act.Fori(0, NT // C) as c:
                act.wait_ge(ln_step, c * (2 * C + 2) + 2 * C + 2)
                act.activation(rstd[:, :], vinv[:, :], ACT.Sqrt).then_inc(root, 1)
                act.wait_ge(zsb_free, c + 1)
                act.wait_ge(att_kept, c + 1)
                for j in range(C + 1):
                    if j < C:
                        act.wait_ge(turned, c * C + j + 1 + C)
                        act.activation(xT[:, j, :], tps[j % 2][:, 0:D], ACT.Copy).then_inc(xT_ready, 1)
                    if j >= 1:
                        act.wait_ge(z_ready, c * C + j)
                        act.activation(zsb[:, j - 1, :], zps[(j - 1) % 2][:, 0:D + 2 * HEADS],
                                       ACT.Copy).then_inc(z_out, 1)

        @block.tensor
        def _(pe):
            pe.sem_inc(turned, C)
            pe.wait_ge(wz_done, 8)

            def project(c, j):
                pe.wait_ge(xT_ready, c * C + j + 3)
                pe.wait_ge(z_out, c * C + (j + 1 if j else 2))
                for k in range(KD):
                    mm = pe.matmul(zps[j % 2][:, 0:D + 2 * HEADS], xT[:, j, k * P:(k + 1) * P], wz[:, k, :],
                                   start=(k == 0), stop=(k == KD - 1))
                mm.then_inc(z_ready, 1)

            with pe.Fori(0, NT // C) as c:
                for j in range(C):
                    pe.wait_ge(xn_ready, c * C + j + 2)
                    pe.wait_ge(xT_ready, c * C + (j + 1 if j else 2))
                    for k in range(KD):
                        mm = pe.transpose(tps[j % 2][:, k * P:(k + 1) * P], xn[:, j, k * P:(k + 1) * P],
                                          K["ident"][:, :])
                    mm.then_inc(turned, 1)
                    if j >= 1:
                        project(c, j - 1)
                project(c, C - 1)


def edge_scores(nc, K, src, dst, es_tab, ed_edge, rec, xd, lo_dram):
    G = 8
    GCOLS = 336
    NG = GCOLS // G
    TCOLS = EC - GCOLS
    TC = 16
    CHUNKS = TCOLS // TC
    PAIRS = TC // 2
    TURN = 112
    HG = 14
    CL = 5
    with ExitStack() as ctx:
        def sb(name, shape, dt=F32):
            return ctx.enter_context(nc.sbuf_tensor(name, shape, dt))

        def sem(name):
            return ctx.enter_context(nc.semaphore(name))

        srcI = sb("srcI", [P, EC + 2 * G], I32)
        dstI = sb("dstI", [P, EC], I32)
        edge0 = sb("edge0", [P, 2], I32)
        pad = sb("pad", [P, EC])
        srcF = sb("srcF", [P, EC + 2 * G])
        part_no = sb("part_no", [P, 1])
        part_noI = sb("part_noI", [P, 1], I32)
        src_lo = sb("src_lo", [P, TCOLS])
        src_hi = sb("src_hi", [P, TCOLS], BF16)
        lo_turned = sb("lo_turned", [TURN, TCOLS // TURN, P], BF16)
        lo_row = sb("lo_row", [P, 2, TC * P], BF16)
        low = sb("low", [P, 2, TC * P], BF16)
        high = sb("high", [P, 2, TC, NT], BF16)
        es_part = sb("es_part", [P, 3, HEADS, NT], BF16)
        masked = sb("masked", [P, TC, HEADS, NT])
        dstF = sb("dstF", [P, EC])
        part = sb("dst_part", [P, 2, EC], I32)
        partB = sb("dst_partB", [P, 2, EC], BF16)
        iotaB = sb("iotaB", [P, P], BF16)
        none = sb("none", [P, P], BF16)
        loHot = sb("loHot", [P, 2, HG, P], BF16)
        hiHot = sb("hiHot", [P, 2, HG, NT], BF16)
        tri = sb("etri", [P, P])
        count = sb("count", [P, NT])
        total = sb("etotal", [P, NT])
        zero = sb("ezero", [P, NT])
        at_node = sb("at_node", [P, NT])
        spare = sb("spare", [P, NT])
        spareI = sb("spareI", [P, NT], I32)
        at_nodeI = sb("at_nodeI", [P, NT], I32)
        before = sb("before", [P, EC])
        after = sb("after", [P, EC])
        goes_on = sb("goes_on", [P, EC])
        idx = sb("idx", [P, 2, G], I32)
        got = sb("got", [P, 2, G, HEADS])
        es = sb("es", [P, HEADS, EC])
        ed = sb("ed", [P, HEADS, EC])
        run = sb("run", [P, HEADS, EC])
        ed_first = run[:, :, :].rearrange("p h t -> p (h t)").rearrange("p (t h) -> p t h", h=HEADS)
        joined = sb("joined", [P, 4])
        ends = sb("ends", [P, 3, 2, HEADS])
        rows = sb("rows", [HEADS, 3, 2, P])
        carried = sb("carried", [HEADS, 3, P + 1])
        first = sb("first", [P, 3, HEADS])
        clear = sb("clear16", [P, CL, 2 * D], F16)
        rest = sb("es_rest", [P, HEADS, NT])
        cps = [ctx.enter_context(nc.psum_tensor(f"cps{b}", [P, 512], F32)) for b in range(4)]
        hist = ctx.enter_context(nc.psum_tensor("hist", [P, 512], F32))
        sums = [ctx.enter_context(nc.psum_tensor(f"sums{b}", [P, 512], F32)) for b in range(2)]
        filled = sem("filled")
        edges_in = sem("edges_in")
        prep = sem("prep")
        copied = sem("src_copied")
        idx_ready = sem("idx_ready")
        landed = [sem(f"landed{s}") for s in range(2)]
        got_out = sem("got_out")
        hot = sem("hot")
        used = sem("hot_used")
        table = sem("es_table")
        lo_ready = sem("lo_ready")
        lo_up = sem("lo_up")
        lo_down = sem("lo_down")
        lo_out = sem("lo_out")
        row_in = [sem(f"row_in{s}") for s in range(2)]
        compared = sem("compared")
        looked_up = sem("looked_up")
        taken = sem("taken")
        reduced = sem("reduced")
        summed = sem("esummed")
        node = sem("node_step")
        placed = sem("ed_placed")
        ed_in = sem("ed_in")
        math = sem("math")
        begun = sem("groups_begun")
        turned = sem("ends_turned")
        exped = sem("exped")
        rec_out = sem("rec_out")
        cleared = sem("xd_cleared")
        block = ctx.enter_context(nc.Block())

        @block.sync
        def _(sp):
            sp.wait_ge(filled, 3)
            for tile, edges in ((srcI, src), (dstI, dst)):
                sp.dma_start(tile[0:FULLP, 0:EC], edges[0:FULLP * EC].rearrange("(p t) -> p t", t=EC)).then_inc(edges_in, 16)
                sp.dma_start(tile[FULLP:P, 0:ETAIL], edges[FULLP * EC:EDGES].rearrange("(p t) -> p t", t=ETAIL)).then_inc(edges_in, 16)
            ahead = dst[0:FULLP * EC].rearrange("(p t) -> p t", t=EC)
            sp.dma_start(edge0[1:P, 0:1], ahead[:, EC - 1:EC], allow_slow_non_contiguous=True).then_inc(edges_in, 16)
            sp.dma_start(edge0[0:FULLP - 1, 1:2], ahead[1:FULLP, 0:1], allow_slow_non_contiguous=True).then_inc(edges_in, 16)
            sp.dma_start(edge0[FULLP - 1:FULLP, 1:2], dst[FULLP * EC:FULLP * EC + 1].rearrange("(p t) -> p t", t=1)).then_inc(edges_in, 16)
            sp.wait_ge(prep, 3)
            sp.wait_ge(copied, 1)
            sp.dma_start(rec[0, :].rearrange("(p t) -> p t", t=EC), srcF[:, 0:EC]).then_inc(rec_out, 16)
            sp.dma_start(rec[1, :].rearrange("(p t) -> p t", t=EC), dstF[:, :]).then_inc(rec_out, 16)
            sp.wait_ge(filled, 5)
            for c in range(XTL * EP // (CL * P)):
                sp.dma_start(xd[c * CL * P:(c + 1) * CL * P, :].rearrange("(t p) d -> p t d", p=P), clear[:, :, :]).then_inc(cleared, 16)
            sp.wait_ge(lo_down, TCOLS // TURN)
            sp.dma_start(lo_dram[0:TCOLS * P].rearrange("(b r p) -> r b p", r=TURN, p=P), lo_turned[:, :, :]).then_inc(lo_out, 16)
            sp.wait_ge(lo_out, 16)

            def row(c, s):
                sp.dma_start(lo_row[:, s, :], lo_dram[bass.ds(c * (TC * P), TC * P)].partition_broadcast(P)).then_inc(row_in[s], 16)

            row(0, 0)
            row(1, 1)
            with sp.Fori(1, CHUNKS // 2) as i:
                for s in range(2):
                    sp.wait_ge(compared, 4 * i + 2 * s - 2)
                    row(2 * i + s, s)
            sp.wait_ge(placed, 16 * NT)
            sp.dma_start(ed_first, ed_edge[0:P * EC, :].rearrange("(p t) h -> p t h", p=P)).then_inc(ed_in, 16)
            for h in range(HEADS):
                sp.wait_ge(exped, h + 1)
                sp.dma_start(rec[2 + h, :].rearrange("(p t) -> p t", t=EC), es[:, h, :]).then_inc(rec_out, 16)
            sp.wait_ge(rec_out, 16 * 6)
            sp.wait_ge(cleared, 16 * (XTL * EP // (CL * P)))

        @block.vector
        def _(dve):
            n = Tally()
            m = Tally()
            p = Tally()

            def then(ins):
                ins.then_inc(math, n.one())
                dve.wait_ge(math, n.n)

            def by_node(ins):
                ins.then_inc(node, m.one())
                dve.wait_ge(node, m.n)

            dve.memset(none[:, :], 0.0).then_inc(node, m.one())
            by_node(dve.memset(zero[:, :], 0.0))
            by_node(dve.tensor_copy(iotaB[:, :], K["iota"][:, :]))
            dve.wait_ge(edges_in, 16 * 7)
            dve.wait_ge(filled, 4)
            dve.tensor_scalar(part[:, 0, 0:TCOLS], srcI[:, GCOLS:EC], P - 1, None, ALU.bitwise_and).then_inc(table, 1)
            dve.tensor_scalar(part[:, 1, 0:TCOLS], srcI[:, GCOLS:EC], 7, None, ALU.arith_shift_right).then_inc(table, 1)
            dve.wait_ge(table, 2)
            dve.tensor_copy(src_lo[:, :], part[:, 0, 0:TCOLS]).then_inc(lo_ready, 1)
            dve.tensor_copy(src_hi[:, :], part[:, 1, 0:TCOLS]).then_inc(table, 1)
            dve.tensor_copy(goes_on[:, :], pad[:, :].bitcast(I32)).then_inc(prep, 1)
            dve.tensor_copy(srcF[:, :], srcI[:, :]).then_inc(copied, 1)
            dve.wait_ge(prep, 1)
            dve.tensor_scalar(goes_on[:, :], goes_on[:, :], float(EDGES), 8192.0, ALU.is_ge, ALU.mult).then_inc(prep, 1)
            dve.wait_ge(prep, 2)
            dve.tensor_tensor(dstF[:, :], dstI[:, :], goes_on[:, :], ALU.add).then_inc(prep, 1)
            dve.wait_ge(prep, 3)
            dve.wait_ge(lo_ready, 1)
            dve.wait_ge(table, 3)
            by_node(dve.tensor_copy(part[:, 0, :], dstF[:, :]))
            by_node(dve.tensor_scalar(part[:, 1, :], part[:, 0, :], P - 1, None, ALU.bitwise_and))
            by_node(dve.tensor_scalar(part[:, 0, :], part[:, 0, :], 7, None, ALU.arith_shift_right))
            by_node(dve.tensor_copy(partB[:, :, :], part[:, :, :]))
            with dve.Fori(0, EC // (2 * HG)) as i:
                for s in range(2):
                    at = (2 * i + s) * HG
                    dve.wait_ge(used, 2 * i + s + 1)
                    for k, (to, width) in enumerate(((hiHot, NT), (loHot, P))):
                        dve.tensor_tensor(to[:, s, :, :], iotaB[:, 0:width].unsqueeze(1).to_broadcast([P, HG, width]),
                                          partB[:, k, bass.ds(at, HG)].unsqueeze(2).to_broadcast([P, HG, width]),
                                          ALU.is_equal).then_inc(hot, 1)
            by_table = Tally()
            by_table.n = 3

            def on_table(ins):
                ins.then_inc(table, by_table.one())
                dve.wait_ge(table, by_table.n)

            es_node = K["att_node"][:, :, 0:HEADS].rearrange("p t h -> p h t")
            on_table(dve.tensor_copy(es_part[:, 0, :, :], es_node))
            on_table(dve.tensor_tensor(rest[:, :, :], es_node, es_part[:, 0, :, :], ALU.subtract))
            on_table(dve.tensor_copy(es_part[:, 1, :, :], rest[:, :, :]))
            on_table(dve.tensor_tensor(rest[:, :, :], rest[:, :, :], es_part[:, 1, :, :], ALU.subtract))
            on_table(dve.tensor_copy(es_part[:, 2, :, :], rest[:, :, :]))
            dve.wait_ge(filled, 8)
            on_table(dve.tensor_copy(part_no[:, :], part_noI[:, :]))
            dve.tensor_tensor(before[:, 1:EC], dstF[:, 1:EC], dstF[:, 0:EC - 1], ALU.not_equal).then_inc(prep, 1)
            dve.tensor_tensor(before[:, 0:1], dstF[:, 0:1], edge0[:, 0:1], ALU.not_equal).then_inc(prep, 1)
            dve.tensor_tensor(after[:, 0:EC - 1], dstF[:, 1:EC], dstF[:, 0:EC - 1], ALU.not_equal).then_inc(prep, 1)
            dve.tensor_tensor(after[:, EC - 1:EC], dstF[:, EC - 1:EC], edge0[:, 1:2], ALU.not_equal).then_inc(prep, 1)
            dve.tensor_tensor(joined[:, 0:1], dstF[:, 0:1], dstF[:, EC - 1:EC], ALU.not_equal).then_inc(prep, 1)
            dve.wait_ge(prep, 8)
            dve.tensor_tensor(joined[:, 1:2], joined[:, 0:1], before[:, 0:1], ALU.max).then_inc(prep, 1)
            dve.tensor_tensor(joined[:, 2:3], joined[:, 0:1], after[:, EC - 1:EC], ALU.max).then_inc(prep, 1)
            dve.tensor_scalar(goes_on[:, :], before[:, :], 0.0, None, ALU.is_equal).then_inc(prep, 1)
            dve.wait_ge(prep, 11)
            dve.tensor_scalar(before[:, :], before[:, :], FAR, None, ALU.mult).then_inc(prep, 1)
            dve.tensor_scalar(after[:, :], after[:, :], FAR, None, ALU.mult).then_inc(prep, 1)
            for h in range(HEADS):
                dve.tensor_scalar(ends[:, 0, 1, h:h + 1], joined[:, 1:2], 0.0, None, ALU.is_equal).then_inc(prep, 1)
                for d in range(2):
                    dve.tensor_scalar(ends[:, 1 + d, 1, h:h + 1], joined[:, 1 + d:2 + d], FAR, None, ALU.mult).then_inc(prep, 1)

            dve.wait_ge(summed, 1)
            by_node(dve.tensor_copy(count[:, :], hist[:, 0:NT]))
            K["count_at"] = m.n
            dve.wait_ge(summed, 2)
            by_node(dve.tensor_copy(total[:, :], sums[1][:, 0:NT]))
            by_node(dve.tensor_tensor_scan(K["start"][:, 0:NT], total[:, :], zero[:, :], 0.0, ALU.add, ALU.add))
            by_node(dve.tensor_tensor(K["start"][:, 0:NT], K["start"][:, 0:NT], total[:, :], ALU.subtract))
            by_node(dve.memset(K["start"][:, NT:NT + 1], EDGES))
            by_node(dve.tensor_tensor(at_node[:, :], K["start"][:, 0:NT], sums[0][:, 0:NT], ALU.add))
            dve.wait_ge(filled, 7)
            by_node(dve.tensor_copy(spare[:, :], spareI[:, :]))
            by_node(dve.tensor_tensor(spare[:, :], spare[:, :], at_node[:, :], ALU.subtract))
            by_node(dve.tensor_scalar(count[:, :], count[:, :], 0.0, None, ALU.is_equal))
            by_node(dve.tensor_tensor(spare[:, :], spare[:, :], count[:, :], ALU.mult))
            by_node(dve.tensor_tensor(at_nodeI[:, :], at_node[:, :], spare[:, :], ALU.add))
            K["placed_at"] = m.n

            K["table_at"] = by_table.n

            def compare(c, s, rounds):
                dve.wait_ge(row_in[s], rounds * 16)
                dve.tensor_scalar(low[:, s, :], lo_row[:, s, :], part_no[:, 0:1], None, ALU.is_equal).then_inc(compared, 1)
                dve.tensor_tensor(high[:, s, :, :], iotaB[:, 0:NT].unsqueeze(1).to_broadcast([P, TC, NT]),
                                  src_hi[:, bass.ds(c * TC, TC)].unsqueeze(2).to_broadcast([P, TC, NT]),
                                  ALU.is_equal).then_inc(compared, 1)

            def take(c, s):
                dve.wait_ge(compared, 2 * c + 2)
                dve.wait_ge(reduced, c + 1)
                for j in range(PAIRS):
                    dve.wait_ge(looked_up, c * PAIRS + j + 1)
                    dve.tensor_tensor(masked[:, 2 * j:2 * j + 2, :, :],
                                      cps[j % 4][:, 0:2 * HEADS * NT].rearrange("p (t h a) -> p t h a", t=2, h=HEADS),
                                      high[:, s, 2 * j:2 * j + 2, :].unsqueeze(2).to_broadcast([P, 2, HEADS, NT]),
                                      ALU.mult).then_inc(taken, 1)
                dve.wait_ge(taken, 4 + (c + 1) * PAIRS)
                dve.tensor_reduce(es[:, :, bass.ds(c * TC + GCOLS, TC)].rearrange("p h g -> p g h"), masked[:, :, :, :],
                                  AX.X, ALU.add).then_inc(reduced, 1)

            dve.sem_inc(taken, 4)
            dve.sem_inc(reduced, 1)
            compare(0, 0, 1)
            with dve.Fori(0, CHUNKS // 2 - 1) as i:
                for s in range(2):
                    compare(2 * i + s + 1, 1 - s, i + (1 + s))
                    take(2 * i + s, s)
            compare(CHUNKS - 1, 1, CHUNKS // 2)
            take(CHUNKS - 2, 0)
            take(CHUNKS - 1, 1)

            def segment_scan(d, keep, data, out, op0, op1, init, step):
                for h in range(HEADS):
                    dve.tensor_tensor_scan(out[h][:, ::step], keep[:, ::step], data[h][:, ::step], init,
                                           op0, op1).then_inc(math, n.one())
                dve.wait_ge(math, n.n)
                end = EC - 1 if step == 1 else 0
                for h in range(HEADS):
                    dve.tensor_copy(ends[:, d, 0, h:h + 1], out[h][:, end:end + 1]).then_inc(math, n.one())
                K["ends_at"].append(n.n)
                dve.memset(carried[:, d, :], init).then_inc(math, n.one())
                dve.wait_ge(turned, 2 * d + 1)
                dve.tensor_copy(rows[:, d, 0, :], cps[0][0:HEADS, 0:P]).then_inc(math, n.one())
                dve.tensor_copy(rows[:, d, 1, :], cps[1][0:HEADS, 0:P]).then_inc(math, n.one())
                dve.wait_ge(math, n.n)
                at = slice(1, P + 1) if step == 1 else slice(P - 1, None, -1)
                dve.tensor_tensor_scan(carried[:, d, at], rows[:, d, 1, ::step], rows[:, d, 0, ::step], init,
                                       op0, op1).then_inc(math, n.one())
                K["carried_at"].append(n.n)
                dve.wait_ge(turned, 2 * d + 2)
                then(dve.tensor_copy(first[:, d, :], cps[2][:, 0:HEADS]))
                for h in range(HEADS):
                    dve.tensor_tensor_scan(out[h][:, ::step], keep[:, ::step], data[h][:, ::step],
                                           first[:, d, h:h + 1], op0, op1).then_inc(math, n.one())
                dve.wait_ge(math, n.n)

            by_head = [[a[:, h, :] for h in range(HEADS)] for a in (es, ed, run)]
            dve.wait_ge(ed_in, 16)
            dve.wait_ge(prep, 25)
            segment_scan(0, goes_on, [ed_first[:, :, h] for h in range(HEADS)], by_head[1], ALU.mult, ALU.add, 0.0, 1)
            dve.wait_ge(got_out, NG)
            dve.wait_ge(reduced, CHUNKS + 1)
            then(dve.tensor_tensor(es[:, :, :], es[:, :, :], ed[:, :, :], ALU.add))
            then(dve.scalar_tensor_tensor(out=es[:, :, :], in0=es[:, :, :], scalar=SLOPE, in1=es[:, :, :],
                                          op0=ALU.mult, op1=ALU.max))
            then(dve.tensor_scalar(ed[:, :, :], es[:, :, :], 0.0, NEG, ALU.is_equal, ALU.mult))
            then(dve.tensor_tensor(es[:, :, :], es[:, :, :], ed[:, :, :], ALU.add))
            segment_scan(1, before, by_head[0], by_head[2], ALU.add, ALU.max, FAR, 1)
            segment_scan(2, after, by_head[2], by_head[1], ALU.add, ALU.max, FAR, -1)
            dve.tensor_tensor(run[:, :, :], es[:, :, :], ed[:, :, :], ALU.subtract).then_inc(math, n.one())
            K["math_end"] = n.n

        @block.gpsimd
        def _(pool):
            pool.memset(srcI[:, :], 0).then_inc(filled, 1)
            pool.memset(dstI[:, :], 0).then_inc(filled, 1)
            pool.memset(edge0[:, :], -1).then_inc(filled, 1)
            pool.iota(pad[:, :].bitcast(I32), pattern=[[1, EC]], base=0, channel_multiplier=EC).then_inc(filled, 1)
            pool.memset(clear[:, :, :], 0.0).then_inc(filled, 1)
            pool.affine_select(out=tri[:, :], in_=K["ones"][:, :], compare_op=ALU.is_gt, fill=0.0,
                               base=0, pattern=[[1, P]], channel_multiplier=-1).then_inc(filled, 1)
            pool.iota(spareI[:, :], pattern=[[P, NT]], base=P * EC, channel_multiplier=1).then_inc(filled, 1)
            pool.iota(part_noI[:, :], pattern=[[1, 1]], base=0, channel_multiplier=1).then_inc(filled, 1)

            def gather(i):
                for s in range(2):
                    pool.wait_ge(idx_ready, 2 * i + s + 1)
                    pool.sem_inc(begun, 1)
                    for g in range(G):
                        pool.indirect_dma_start(
                            out=got[:, s, g, :], out_offset=None, in_=es_tab[:, :],
                            in_offset=bass.IndirectOffsetOnAxis(ap=idx[:, s, g:g + 1], axis=0)).then_inc(landed[s], 16)

            with pool.Fori(0, NG // 4) as i:
                gather(i)
            pool.wait_ge(node, K["placed_at"])
            for w in range(NT):
                pool.indirect_dma_start(
                    out=ed_edge[:, :], out_offset=bass.IndirectOffsetOnAxis(ap=at_nodeI[:, w:w + 1], axis=0),
                    in_=K["att_node"][:, w, HEADS:2 * HEADS], in_offset=None).then_inc(placed, 16)
            with pool.Fori(NG // 4, NG // 2) as i:
                gather(i)

        @block.scalar
        def _(act):
            act.wait_ge(copied, 1)
            for b in range(TCOLS // TURN):
                act.wait_ge(lo_up, b + 1)
                act.activation(lo_turned[:, b, :], cps[b][0:TURN, 0:P], ACT.Copy).then_inc(lo_down, 1)
            for s in range(2):
                act.activation(idx[:, s, :], srcF[:, s * G:(s + 1) * G], ACT.Copy).then_inc(idx_ready, 1)
            with act.Fori(0, NG // 2) as i:
                for s in range(2):
                    act.wait_ge(landed[s], i * (G * 16) + G * 16)
                    at = (2 * i + s) * G
                    act.activation(es[:, :, bass.ds(at, G)].rearrange("p h g -> p g h"), got[:, s, :, :], ACT.Copy).then_inc(got_out, 1)
                    act.wait_ge(got_out, 2 * i + s + 1)
                    act.activation(idx[:, s, :], srcF[:, bass.ds(at + 2 * G, G)], ACT.Copy).then_inc(idx_ready, 1)
            act.wait_ge(math, K["math_end"])
            for h in range(HEADS):
                act.activation(es[:, h, :], run[:, h, :], ACT.Exp).then_inc(exped, 1)

        @block.tensor
        def _(pe):
            pe.sem_inc(used, 2)
            pe.wait_ge(lo_ready, 1)
            for b in range(TCOLS // TURN):
                pe.transpose(cps[b][0:TURN, 0:P], src_lo[:, b * TURN:(b + 1) * TURN], K["ident"][:, :]).then_inc(lo_up, 1)
            pe.wait_ge(node, 3)
            pe.matmul(hist[:, 0:NT], none[:, :], none[:, 0:NT], start=True, stop=False)
            with pe.Fori(0, EC // (2 * HG)) as i:
                for s in range(2):
                    pe.wait_ge(hot, 4 * i + 2 * s + 2)
                    for j in range(HG):
                        mm = pe.matmul(hist[:, 0:NT], loHot[:, s, j, :], hiHot[:, s, j, :], start=False, stop=False)
                    mm.then_inc(used, 1)
            pe.matmul(hist[:, 0:NT], none[:, :], none[:, 0:NT], start=False, stop=True).then_inc(summed, 1)
            pe.wait_ge(node, K["count_at"])
            pe.wait_ge(filled, 6)
            pe.matmul(sums[0][:, 0:NT], tri[:, :], count[:, :], start=True, stop=True)
            pe.matmul(sums[1][:, 0:NT], K["ones"][:, :], count[:, :], start=True, stop=True).then_inc(summed, 1)
            pe.wait_ge(table, K["table_at"])
            pe.wait_ge(lo_down, TCOLS // TURN)
            with pe.Fori(0, CHUNKS // 2) as i:
                for s in range(2):
                    c = 2 * i + s
                    pe.wait_ge(compared, 2 * c + 2)
                    for j in range(PAIRS):
                        pe.wait_ge(taken, c * PAIRS + j + 1)
                        for t in range(2):
                            edges = low[:, s, (2 * j + t) * P:(2 * j + t + 1) * P]
                            for k in range(3):
                                mm = pe.matmul(cps[j % 4][:, t * HEADS * NT:(t + 1) * HEADS * NT], edges,
                                               es_part[:, k, :, :].rearrange("p h a -> p (h a)"), start=(k == 0), stop=(k == 2))
                        mm.then_inc(looked_up, 1)
            pe.wait_ge(prep, 25)
            for d, backwards in enumerate((False, False, True)):
                pe.wait_ge(math, K["ends_at"][d])
                pe.transpose(cps[0][0:HEADS, 0:P], ends[:, d, 0, :], K["ident"][:, :])
                pe.transpose(cps[1][0:HEADS, 0:P], ends[:, d, 1, :], K["ident"][:, :]).then_inc(turned, 1)
                pe.wait_ge(math, K["carried_at"][d])
                at = slice(1, P + 1) if backwards else slice(0, P)
                pe.transpose(cps[2][:, 0:HEADS], carried[:, d, at], K["ident"][0:HEADS, 0:HEADS]).then_inc(turned, 1)


def plan_visits(nc, K, rec, wtab):
    with ExitStack() as ctx:
        def sb(name, shape, dt=F32):
            return ctx.enter_context(nc.sbuf_tensor(name, shape, dt))

        def sem(name):
            return ctx.enter_context(nc.semaphore(name))

        start = K["start"]
        startI = sb("startI", [P, 2, NT + 1], I32)
        tiles = sb("tiles", [P, 2, NT + 1])
        many = sb("many", [P, NT])
        manyI = sb("manyI", [P, NT], I32)
        vend = sb("vend", [P, NT])
        zero = sb("zero", [P, NT])
        shift = sb("shift", [P, NT])
        vI = sb("vI", [P, VB], I32)
        v = sb("v", [P, VB])
        mask = sb("mask", [P, VB, NT])
        wv = sb("wv", [P, VB])
        w0 = sb("w0", [P, VB])
        wI = sb("wI", [P, VB], I32)
        tv = sb("tv", [P, VB])
        tI = sb("tI", [P, 6, VB], I32)
        tF = sb("tF", [P, 6, VB])
        vr = sb("vr", [P, 6, VB, P])
        vps = [ctx.enter_context(nc.psum_tensor(f"vps{b}", [P, 512], F32)) for b in range(4)]
        ramp = sem("v_ramp")
        step = sem("plan_step")
        planned = sem("planned")
        fetched = sem("fetched")
        local = sem("local")
        turned = sem("visits_turned")
        laid = sem("laid")
        table = sem("table")
        block = ctx.enter_context(nc.Block())

        @block.gpsimd
        def _(pool):
            pool.iota(vI[:, :], pattern=[[P, VB]], base=0, channel_multiplier=1).then_inc(ramp, 1)
            pool.wait_ge(planned, 1)
            for k in range(6):
                for b in range(VB):
                    pool.indirect_dma_start(
                        out=vr[:, k, b, :], out_offset=None, in_=rec.rearrange("k (t e) -> (k t) e", e=P),
                        in_offset=bass.IndirectOffsetOnAxis(ap=tI[:, k, b:b + 1], axis=0)).then_inc(fetched, 16)

        @block.tensor
        def _(pe):
            pe.wait_ge(fetched, 16 * 6 * VB)
            pe.wait_ge(local, VB)
            for k in range(6):
                for b in range(VB):
                    m = k * VB + b
                    if m >= 4:
                        pe.wait_ge(laid, m - 3)
                    pe.transpose(vps[m % 4][:, 0:P], vr[:, k, b, :], K["ident"][:, :]).then_inc(turned, 1)

        @block.scalar
        def _(act):
            for m in range(6 * VB):
                k, b = m // VB, m % VB
                act.wait_ge(turned, m + 1)
                to = (K["srcV"], K["dstV"])[k][:, b * P:(b + 1) * P] if k < 2 else K["exV"][:, b * P:(b + 1) * P, k - 2]
                act.activation(to, vps[m % 4][:, 0:P], ACT.Copy).then_inc(laid, 1)

        @block.sync
        def _(sp):
            sp.wait_ge(planned, 1)
            sp.dma_start(wtab.rearrange("(b p) -> p b", p=P), wI[:, :], allow_slow_non_contiguous=True).then_inc(table, 16)
            sp.wait_ge(table, 16)
            sp.dma_start(K["wrow"][:, :], wtab.rearrange("(a v) -> a v", a=1)).then_inc(table, 16)
            sp.wait_ge(table, 32)

        @block.vector
        def _(dve):
            n = Tally()

            def after(ins):
                ins.then_inc(step, n.one())
                dve.wait_ge(step, n.n)

            after(dve.memset(zero[:, :], 0.0))
            dve.wait_ge(ramp, 1)
            after(dve.tensor_copy(v[:, :], vI[:, :]))
            after(dve.tensor_copy(startI[:, 0, :], start[:, :]))
            after(dve.tensor_scalar(startI[:, 1, :], start[:, :], float(P - 1), None, ALU.add))
            after(dve.tensor_scalar(startI[:, :, :], startI[:, :, :], 7, None, ALU.arith_shift_right))
            after(dve.tensor_copy(tiles[:, :, :], startI[:, :, :]))
            after(dve.tensor_tensor(many[:, :], tiles[:, 1, 1:NT + 1], tiles[:, 0, 0:NT], ALU.subtract))
            after(dve.tensor_scalar(manyI[:, :], many[:, :], 1.0, None, ALU.add))
            after(dve.tensor_scalar(manyI[:, :], manyI[:, :], -2, None, ALU.bitwise_and))
            after(dve.tensor_copy(many[:, :], manyI[:, :]))
            after(dve.tensor_tensor_scan(vend[:, :], many[:, :], zero[:, :], 0.0, ALU.add, ALU.add))
            after(dve.tensor_tensor(shift[:, :], many[:, :], vend[:, :], ALU.subtract))
            after(dve.tensor_tensor(shift[:, :], shift[:, :], tiles[:, 0, 0:NT], ALU.add))
            whole = [P, VB, NT]
            after(dve.tensor_tensor(mask[:, :, :], vend[:, :].unsqueeze(1).to_broadcast(whole),
                                    v[:, :].unsqueeze(2).to_broadcast(whole), ALU.is_le))
            after(dve.tensor_reduce(wv[:, :], mask[:, :, :], AX.X, ALU.add))
            after(dve.tensor_tensor(mask[:, :, :], K["iota"][:, 0:NT].unsqueeze(1).to_broadcast(whole),
                                    wv[:, :].unsqueeze(2).to_broadcast(whole), ALU.is_equal))
            after(dve.tensor_tensor(mask[:, :, :], mask[:, :, :], shift[:, :].unsqueeze(1).to_broadcast(whole), ALU.mult))
            after(dve.tensor_reduce(tv[:, :], mask[:, :, :], AX.X, ALU.add))
            after(dve.tensor_tensor(tv[:, :], tv[:, :], v[:, :], ALU.add))
            after(dve.tensor_scalar(wI[:, :], wv[:, :], float(NT - 1), None, ALU.min))
            after(dve.tensor_scalar(w0[:, :], wv[:, :], float(P), None, ALU.mult))
            for k in range(6):
                after(dve.tensor_scalar(tF[:, k, :], tv[:, :], float(ETILES - 1), float(k * ETILES), ALU.min, ALU.add))
            dve.tensor_copy(tI[:, :, :], tF[:, :, :]).then_inc(planned, 1)
            dve.wait_ge(fetched, 16 * 6 * VB)
            for b in range(VB):
                dve.tensor_scalar(vr[:, 1, b, :], vr[:, 1, b, :], w0[:, b:b + 1], None, ALU.subtract).then_inc(local, 1)


def aggregate(nc, K, zt):
    PAIRS, SLOTS = 2, 4
    G = 2 * PAIRS
    GROUPS = VISITS // G
    with ExitStack() as ctx:
        def sb(name, shape, dt=F32):
            return ctx.enter_context(nc.sbuf_tensor(name, shape, dt))

        def sem(name):
            return ctx.enter_context(nc.semaphore(name))

        acc = sb("acc", [P, NT, ZW])
        idx = sb("vidx", [P, SLOTS, G], I32)
        z = sb("z", [P, SLOTS, G, ZW])
        hot = sb("hot", [P, SLOTS, G, P])
        rden = sb("rden", [P, NT, HEADS])
        ups = [ctx.enter_context(nc.psum_tensor(f"ups{b}", [P, 512], F32)) for b in range(SLOTS * PAIRS)]
        idx_ready = sem("vidx_ready")
        landed = [sem(f"z_landed{s}") for s in range(SLOTS)]
        scaled = sem("scaled")
        ex_in = sem("ex_in")
        summed = sem("summed")
        added = sem("added")
        begun = sem("visit_groups_begun")
        fin = sem("gnn_fin")
        block = ctx.enter_context(nc.Block())

        @block.gpsimd
        def _(pool):
            with pool.Fori(0, GROUPS // SLOTS) as i:
                for s in range(SLOTS):
                    pool.wait_ge(idx_ready, i * SLOTS + s + 1)
                    pool.wait_ge(summed, i * SLOTS + s + 1)
                    pool.sem_inc(begun, 1)
                    for g in range(G):
                        pool.indirect_dma_start(
                            out=z[:, s, g, 0:D], out_offset=None, in_=zt[:, :],
                            in_offset=bass.IndirectOffsetOnAxis(ap=idx[:, s, g:g + 1], axis=0)).then_inc(landed[s], 16)

        @block.scalar
        def _(act):
            for s in range(SLOTS):
                act.activation(idx[:, s, :], K["srcV"][:, s * G:(s + 1) * G], ACT.Copy).then_inc(idx_ready, 1)
            with act.Fori(0, GROUPS // SLOTS) as i:
                for s in range(SLOTS):
                    first = (i * SLOTS + s) * G
                    act.wait_ge(landed[s], i * (16 * G) + 16 * G)
                    act.activation(z[:, s, :, D:ZW], K["exV"][:, bass.ds(first, G), :], ACT.Copy).then_inc(ex_in, 1)
                    act.activation(idx[:, s, :], K["srcV"][:, bass.ds(first + SLOTS * G, G)], ACT.Copy).then_inc(idx_ready, 1)

        @block.vector
        def _(dve):
            dve.memset(acc[:, :, :], 0.0).then_inc(fin, 1)
            dve.wait_ge(fin, 1)
            dve.sem_inc(added, SLOTS * PAIRS)

            def scale(group, s, rounds):
                dve.wait_ge(landed[s], rounds * (16 * G))
                ex = K["exV"][:, bass.ds(group * G, G), :]
                heads = z[:, s, :, 0:D].rearrange("p g (h f) -> p g h f", h=HEADS)
                dve.tensor_tensor(heads, heads, ex.unsqueeze(3).to_broadcast([P, G, HEADS, FH]), ALU.mult).then_inc(scaled, 1)

            def one_hot(group, s):
                dve.tensor_tensor(hot[:, s, :, :], K["iota"][:, :].unsqueeze(1).to_broadcast([P, G, P]),
                                  K["dstV"][:, bass.ds(group * G, G)].unsqueeze(2).to_broadcast([P, G, P]),
                                  ALU.is_equal).then_inc(scaled, 1)

            def accumulate(group, s, pair, window):
                dve.wait_ge(summed, group + 1 + SLOTS)
                dve.wait_ge(added, group * PAIRS + (pair + SLOTS * PAIRS))
                into = acc[:, bass.ds(window, 1), :].rearrange("p a z -> p (a z)")
                dve.tensor_tensor(into, ups[s * PAIRS + pair][:, 0:ZW], into, ALU.add).then_inc(added, 1)

            def step(group, s, rounds):
                windows = [dve.value_load(K["wrow"][0:1, bass.ds(group * G + 2 * pair, 1)]) for pair in range(PAIRS)]
                if rounds is not None:
                    scale(group + 1, (s + 1) % SLOTS, rounds)
                    one_hot(group + 1, (s + 1) % SLOTS)
                for pair in range(PAIRS):
                    accumulate(group, s, pair, windows[pair])

            scale(0, 0, 1)
            one_hot(0, 0)
            with dve.Fori(0, GROUPS // SLOTS - 1) as i:
                for s in range(SLOTS):
                    step(i * SLOTS + s, s, i + ((s + 1) // SLOTS + 1))
            for s in range(SLOTS):
                step(GROUPS - SLOTS + s, s, GROUPS // SLOTS if s < SLOTS - 1 else None)
            dve.wait_ge(added, GROUPS * PAIRS + SLOTS * PAIRS)
            dve.tensor_scalar(rden[:, :, :], acc[:, :, D:ZW], 1e-30, None, ALU.max).then_inc(fin, 1)
            dve.wait_ge(fin, 2)
            dve.reciprocal(rden[:, :, :], rden[:, :, :]).then_inc(fin, 1)
            dve.wait_ge(fin, 3)
            for h in range(HEADS):
                part = acc[:, :, h * FH:(h + 1) * FH]
                dve.tensor_tensor(part, part, rden[:, :, h:h + 1].to_broadcast([P, NT, FH]), ALU.mult).then_inc(fin, 1)
            dve.wait_ge(fin, 7)
            dve.tensor_tensor(K["x2"][:, :, :], K["x2"][:, :, :], acc[:, :, 0:D], ALU.add)

        @block.tensor
        def _(pe):
            pe.sem_inc(summed, SLOTS)
            with pe.Fori(0, GROUPS // SLOTS) as i:
                for s in range(SLOTS):
                    group = i * SLOTS + s
                    pe.wait_ge(scaled, 2 * group + 2)
                    pe.wait_ge(ex_in, group + 1)
                    pe.wait_ge(added, group * PAIRS + PAIRS)
                    for g in range(G):
                        mm = pe.matmul(ups[s * PAIRS + g // 2][:, 0:ZW], hot[:, s, g, :], z[:, s, g, :],
                                       start=(g % 2 == 0), stop=(g % 2 == 1))
                    mm.then_inc(summed, 1)


def route(nc, K, Wr, br, xd):
    C = 7
    with ExitStack() as ctx:
        def sb(name, shape, dt=F32):
            return ctx.enter_context(nc.sbuf_tensor(name, shape, dt))

        def sem(name):
            return ctx.enter_context(nc.semaphore(name))

        X = K["x2"]
        wr = sb("wr", [P, KD, NE])
        brb = sb("brb", [P, NE])
        tri = sb("tri", [P, P])
        stats = sb("rstats", [P, C, 6])
        mv = sb("rmv", [P, C, 2])
        vinv = sb("rvinv", [P, C])
        rstd = sb("rrstd", [P, C])
        inner = sb("inner", [P, C])
        rin = sb("rin", [P, C])
        xt = sb("xt", [P, C, D])
        xT = sb("rxT", [P, C, D])
        lg = sb("lg", [P, NT, NE])
        tmp = sb("rtmp", [P, NT, NE])
        hot = [sb(f"chosen{k}", [P, NT, NE]) for k in range(2)]
        both = sb("both", [P, NT, NE])
        place = sb("place", [P, NT, NE])
        zero = sb("rzero", [P, NT])
        top = sb("top", [P, 2, NT])
        pick = sb("pick", [P, NT])
        p2 = sb("p2", [P, NT])
        total = sb("total", [P, NT, NE])
        upto = sb("upto", [P, NT, NE])
        ntile = sb("ntile", [P, NE])
        ntileI = sb("ntileI", [P, NE], I32)
        tend = sb("tend", [P, NE])
        base = sb("base", [P, NE])
        tmask = sb("tmask", [1, P, NE])
        trow = sb("trow", [1, P])
        tps = [ctx.enter_context(nc.psum_tensor(f"rtps{b}", [P, 512], F32)) for b in range(2)]
        lps = ctx.enter_context(nc.psum_tensor("lps", [P, 512], F32))
        cps = [ctx.enter_context(nc.psum_tensor(f"rcps{b}", [P, 512], F32)) for b in range(2)]
        par_in = sem("par_in")
        x2_out = sem("x2_out")
        tri_done = sem("tri_done")
        ln_step = sem("rln_step")
        root = sem("rroot")
        begun = sem("raggregation_begun")
        xt_ready = sem("xt_ready")
        turned = sem("rturned")
        xT_ready = sem("rxT_ready")
        lg_ready = sem("lg_ready")
        lg_out = sem("lg_out")
        step = sem("route_step")
        p2_done = sem("p2_done")
        counted = sem("rcounted")
        block = ctx.enter_context(nc.Block())
        L = 2 * C + 4

        @block.sync
        def _(sp):
            for c in range(NT // C):
                sp.dma_start(K["x2d"][c * C * P:(c + 1) * C * P, :].rearrange("(t p) d -> p t d", p=P),
                             X[:, c * C:(c + 1) * C, :]).then_inc(x2_out, 16)
            sp.dma_start(wr[:, :, :], Wr.rearrange("(k p) e -> p k e", p=P)).then_inc(par_in, 16)
            sp.dma_start(brb[:, :], br.partition_broadcast(P)).then_inc(par_in, 16)
            sp.wait_ge(x2_out, 16 * (NT // C))

        @block.gpsimd
        def _(pool):
            pool.affine_select(out=tri[:, :], in_=K["ones"][:, :], compare_op=ALU.is_gt, fill=0.0,
                               base=0, pattern=[[1, P]], channel_multiplier=-1).then_inc(tri_done, 1)

        @block.vector
        def _(dve):
            dve.sem_inc(xt_ready, 1)
            with dve.Fori(0, NT // C) as c:
                dve.wait_ge(xt_ready, c * C + 1)
                for j in range(C):
                    dve.bn_stats(stats[:, j, :], X[:, c * C + j, :]).then_inc(ln_step, 1)
                dve.wait_ge(ln_step, c * L + C)
                dve.sem_inc(begun, 1)
                for j in range(C):
                    dve.bn_aggr(mv[:, j, :], stats[:, j, :]).then_inc(ln_step, 1)
                dve.wait_ge(ln_step, c * L + 2 * C)
                dve.tensor_scalar(vinv[:, :], mv[:, :, 1], EPS, None, ALU.add).then_inc(ln_step, 1)
                dve.wait_ge(ln_step, c * L + 2 * C + 1)
                dve.reciprocal(vinv[:, :], vinv[:, :]).then_inc(ln_step, 1)
                dve.wait_ge(ln_step, c * L + 2 * C + 2)
                dve.tensor_tensor(inner[:, :], mv[:, :, 1], vinv[:, :], ALU.mult).then_inc(ln_step, 1)
                dve.wait_ge(ln_step, c * L + 2 * C + 3)
                dve.tensor_scalar(inner[:, :], inner[:, :], EPS, None, ALU.add).then_inc(ln_step, 1)
                dve.wait_ge(ln_step, c * L + 2 * C + 4)
                dve.reciprocal(inner[:, :], inner[:, :]).then_inc(step, 1)
                dve.wait_ge(root, 2 * c + 2)
                dve.tensor_copy(K["mean"][:, bass.ds(c * C, C)], mv[:, :, 0]).then_inc(step, 1)
                dve.tensor_tensor(K["rstd"][:, bass.ds(c * C, C)], rstd[:, :], rin[:, :], ALU.mult).then_inc(step, 1)
                dve.wait_ge(step, c * 3 + 3)
                for j in range(C):
                    dve.wait_ge(turned, c * C + j + 1)
                    dve.tensor_scalar(xt[:, j, :], X[:, c * C + j, :], mv[:, j, 0:1], rstd[:, j:j + 1],
                                      ALU.subtract, ALU.mult).then_inc(xt_ready, 1)
            n = Tally()
            n.n = 3 * (NT // C)

            def after(ins):
                ins.then_inc(step, n.one())
                dve.wait_ge(step, n.n)

            whole = [P, NT, NE]
            number = K["iota"][:, 0:NE].unsqueeze(1).to_broadcast(whole)
            after(dve.memset(zero[:, :], 0.0))
            dve.wait_ge(lg_out, NT // C + 1)
            dve.wait_ge(par_in, 32)
            after(dve.tensor_tensor(lg[:, :, :], lg[:, :, :], brb[:, :].unsqueeze(1).to_broadcast(whole), ALU.add))
            for k in range(2):
                after(dve.tensor_reduce(top[:, k, :], lg[:, :, :], AX.X, ALU.max))
                after(dve.tensor_tensor(tmp[:, :, :], lg[:, :, :], top[:, k, :].unsqueeze(2).to_broadcast(whole), ALU.not_equal))
                after(dve.scalar_tensor_tensor(out=tmp[:, :, :], in0=tmp[:, :, :], scalar=float(NE), in1=number,
                                               op0=ALU.mult, op1=ALU.add))
                after(dve.tensor_reduce(pick[:, :], tmp[:, :, :], AX.X, ALU.min))
                after(dve.tensor_tensor(hot[k][:, :, :], number, pick[:, :].unsqueeze(2).to_broadcast(whole), ALU.is_equal))
                if k == 0:
                    after(dve.scalar_tensor_tensor(out=lg[:, :, :], in0=hot[0][:, :, :], scalar=FAR, in1=lg[:, :, :],
                                                   op0=ALU.mult, op1=ALU.add))
            after(dve.tensor_tensor(both[:, :, :], hot[0][:, :, :], hot[1][:, :, :], ALU.add))
            dve.wait_ge(tri_done, 1)
            after(dve.tensor_scalar(both[:, NT - 1, :], both[:, NT - 1, :], tri[:, TAIL:TAIL + 1], None, ALU.mult))
            K["both_at"] = n.n
            after(dve.tensor_tensor(pick[:, :], top[:, 1, :], top[:, 0, :], ALU.subtract))
            K["pick_at"] = n.n
            dve.wait_ge(p2_done, 1)
            after(dve.tensor_scalar(K["gate"][:, 0, :], p2[:, :], 1.0, None, ALU.add))
            after(dve.reciprocal(K["gate"][:, 0, :], K["gate"][:, 0, :]))
            after(dve.tensor_tensor(K["gate"][:, 1, :], p2[:, :], K["gate"][:, 0, :], ALU.mult))
            dve.wait_ge(counted, 1)
            after(dve.tensor_copy(total[:, :, :], cps[1][:, 0:NT * NE].rearrange("p (t e) -> p t e", e=NE)))
            for e in range(NE):
                after(dve.tensor_tensor_scan(upto[:, :, e], total[:, :, e], zero[:, :], 0.0, ALU.add, ALU.add))
            after(dve.tensor_scalar(ntileI[:, :], upto[:, NT - 1, :], float(EP - 1), None, ALU.add))
            after(dve.tensor_scalar(ntileI[:, :], ntileI[:, :], 8, None, ALU.arith_shift_right))
            after(dve.tensor_copy(ntile[:, :], ntileI[:, :]))
            after(dve.tensor_tensor_scan(tend[:, :], ntile[:, :], zero[:, 0:NE], 0.0, ALU.add, ALU.add))
            after(dve.tensor_tensor(base[:, :], tend[:, :], ntile[:, :], ALU.subtract))
            after(dve.tensor_scalar(base[:, :], base[:, :], float(EP), None, ALU.mult))
            after(dve.tensor_tensor(place[:, :, :], upto[:, :, :], total[:, :, :], ALU.subtract))
            after(dve.tensor_tensor(place[:, :, :], place[:, :, :],
                                    cps[0][:, 0:NT * NE].rearrange("p (t e) -> p t e", e=NE), ALU.add))
            after(dve.tensor_tensor(place[:, :, :], place[:, :, :], base[:, :].unsqueeze(1).to_broadcast(whole), ALU.add))
            for k in range(2):
                after(dve.tensor_tensor(hot[k][:, :, :], hot[k][:, :, :], place[:, :, :], ALU.mult))
                after(dve.tensor_reduce(pick[:, :], hot[k][:, :, :], AX.X, ALU.add))
                after(dve.tensor_copy(K["slot"][:, k, 0:NT], pick[:, :]))
            tw = [1, P, NE]
            after(dve.tensor_tensor(tmask[:, :, :], tend[0:1, :].unsqueeze(1).to_broadcast(tw),
                                    K["iota"][0:1, :].unsqueeze(2).to_broadcast(tw), ALU.is_le))
            after(dve.tensor_reduce(trow[:, :], tmask[:, :, :], AX.X, ALU.add))
            after(dve.tensor_scalar(K["erow"][:, :], trow[:, :], float(NE - 1), None, ALU.min))

        @block.scalar
        def _(act):
            act.sem_inc(xT_ready, 2)
            act.sem_inc(lg_out, 1)
            with act.Fori(0, NT // C) as c:
                act.wait_ge(ln_step, c * L + 2 * C + 2)
                act.activation(rstd[:, :], vinv[:, :], ACT.Sqrt).then_inc(root, 1)
                act.wait_ge(step, c * 3 + 1)
                act.activation(rin[:, :], inner[:, :], ACT.Sqrt).then_inc(root, 1)
                for j in range(C):
                    act.wait_ge(turned, c * C + j + 1 + C)
                    act.activation(xT[:, j, :], tps[j % 2][:, 0:D], ACT.Copy).then_inc(xT_ready, 1)
                act.wait_ge(lg_ready, c * C + C)
                act.activation(lg[:, bass.ds(c * C, C), :], lps[:, 0:C * NE].rearrange("p (t e) -> p t e", e=NE),
                               ACT.Copy).then_inc(lg_out, 1)
            act.wait_ge(step, K["pick_at"])
            act.activation(p2[:, :], pick[:, :], ACT.Exp).then_inc(p2_done, 1)

        @block.tensor
        def _(pe):
            pe.sem_inc(turned, C)
            pe.wait_ge(par_in, 32)
            with pe.Fori(0, NT // C) as c:
                for j in range(C):
                    pe.wait_ge(xt_ready, c * C + j + 2)
                    pe.wait_ge(xT_ready, c * C + (j + 1 if j else 2))
                    for k in range(KD):
                        mm = pe.transpose(tps[j % 2][:, k * P:(k + 1) * P], xt[:, j, k * P:(k + 1) * P],
                                          K["ident"][:, :])
                    mm.then_inc(turned, 1)
                pe.wait_ge(lg_out, c + 1)
                for j in range(C):
                    pe.wait_ge(xT_ready, c * C + j + 3)
                    for k in range(KD):
                        mm = pe.matmul(lps[:, j * NE:(j + 1) * NE], xT[:, j, k * P:(k + 1) * P], wr[:, k, :],
                                       start=(k == 0), stop=(k == KD - 1))
                    mm.then_inc(lg_ready, 1)
            pe.wait_ge(tri_done, 1)
            pe.wait_ge(step, K["both_at"])
            flat = both[:, :, :].rearrange("p t e -> p (t e)")
            pe.matmul(cps[0][:, 0:NT * NE], tri[:, :], flat, start=True, stop=True)
            pe.matmul(cps[1][:, 0:NT * NE], K["ones"][:, :], flat, start=True, stop=True).then_inc(counted, 1)


def dispatch(nc, K, xd):
    C = 7
    with ExitStack() as ctx:
        def sb(name, shape, dt=F32):
            return ctx.enter_context(nc.sbuf_tensor(name, shape, dt))

        def sem(name):
            return ctx.enter_context(nc.semaphore(name))

        xn = sb("dxn", [P, C, D])
        parts = sb("parts", [P, C, 2 * D], F16)
        idx = sb("didx", [P, C, 2], I32)
        normed = sem("normed")
        split = sem("split")
        sent = [sem(f"sent{j}") for j in range(C)]
        begun = sem("dispatch_begun")
        block = ctx.enter_context(nc.Block())

        def send(pool, j, rows):
            for k in range(2):
                pool.indirect_dma_start(
                    out=xd[:, :], out_offset=bass.IndirectOffsetOnAxis(ap=idx[0:rows, j, k:k + 1], axis=0),
                    in_=parts[0:rows, j, :], in_offset=None).then_inc(sent[j], 16)

        @block.vector
        def _(dve):
            def chunk(c, first=False):
                for j in range(C):
                    t = c * C + j
                    dve.tensor_scalar(xn[:, j, :], K["x2"][:, t, :], K["mean"][:, bass.ds(t, 1)], K["rstd"][:, bass.ds(t, 1)],
                                      ALU.subtract, ALU.mult).then_inc(normed, 1)
                for j in range(C):
                    t = c * C + j
                    if not first:
                        dve.wait_ge(sent[j], 32 * c)
                    dve.tensor_copy(idx[:, j, :], K["slot"][:, :, bass.ds(t, 1)].rearrange("p k a -> p (k a)")).then_inc(split, 1)
                    dve.wait_ge(normed, t + 1)
                    dve.tensor_copy(parts[:, j, 0:D], xn[:, j, :]).then_inc(split, 1)
                    dve.wait_ge(split, 3 * t + 2)
                    dve.tensor_tensor(parts[:, j, D:2 * D], xn[:, j, :], parts[:, j, 0:D], ALU.subtract).then_inc(split, 1)
                dve.wait_ge(split, 3 * C * (c + 1))

            chunk(0, first=True)
            with dve.Fori(1, NT // C) as c:
                chunk(c)

        @block.gpsimd
        def _(pool):
            with pool.Fori(0, NT // C - 1) as c:
                for j in range(C):
                    pool.wait_ge(split, 3 * (c * C + j + 1))
                    pool.sem_inc(begun, 1)
                    send(pool, j, P)
            for j in range(C):
                pool.wait_ge(split, 3 * (NT - C + j + 1))
                send(pool, j, P if j < C - 1 else TAIL)
            for j in range(C):
                pool.wait_ge(sent[j], 32 * (NT // C))


def prepare_weights(nc, K, ln_g, ln_b, W1, b1, W2, b2):
    with ExitStack() as ctx:
        def sb(name, shape, dt=F32):
            return ctx.enter_context(nc.sbuf_tensor(name, shape, dt))

        def sem(name):
            return ctx.enter_context(nc.semaphore(name))

        stage = sb("stage", [P, 2, KD * HID])
        rowsb1 = sb("rowsb1", [NE * MH, P])
        rowsln = sb("rowsln", [2 * NE * KD, P])
        lnT = sb("lnT", [P, 2, NE, KD])
        gain = sb("gain", [P, NE, KD])
        b1T = sb("b1T", [P, NE, MH])
        tps = ctx.enter_context(nc.psum_tensor("wtps", [P, 512], F32))
        bps = [ctx.enter_context(nc.psum_tensor(f"bps{s}", [P, 512], F32)) for s in range(2)]
        small_in = sem("small_in")
        raw_in = [sem(f"raw_in{s}") for s in range(2)]
        small = sem("small")
        turned = sem("wturned")
        hi = sem("hi")
        lo = sem("lo")
        biased = sem("biased")
        bias_out = sem("bias_out")
        block = ctx.enter_context(nc.Block())

        @block.sync
        def _(sp):
            sp.dma_start(rowsb1[:, :], b1.rearrange("e (m p) -> (e m) p", p=P)).then_inc(small_in, 16)
            sp.dma_start(rowsln[0:NE * KD, :], ln_g.rearrange("e (k p) -> (e k) p", p=P)).then_inc(small_in, 16)
            sp.dma_start(rowsln[NE * KD:2 * NE * KD, :], ln_b.rearrange("e (k p) -> (e k) p", p=P)).then_inc(small_in, 16)
            sp.dma_start(K["b2b"][:, :, :], b2.partition_broadcast(P)).then_inc(small_in, 16)
            with sp.Fori(0, NE) as e:
                sp.wait_ge(lo, 3 * e + 1)
                sp.dma_start(stage[:, 0, :].rearrange("p (k h) -> p k h", k=KD),
                             W1[bass.ds(e, 1), :, :].rearrange("a (k p) h -> p (a k) h", p=P)).then_inc(raw_in[0], 16)
                sp.dma_start(stage[:, 1, :].rearrange("p (m d) -> p m d", m=MH),
                             W2[bass.ds(e, 1), :, :].rearrange("a (m p) d -> p (a m) d", p=P)).then_inc(raw_in[1], 16)
            sp.wait_ge(small_in, 64)

        @block.tensor
        def _(pe):
            pe.wait_ge(small_in, 64)
            pe.transpose(tps[:, 0:NE * MH], rowsb1[:, :], K["ident"][0:NE * MH, 0:NE * MH])
            pe.transpose(tps[:, 64:64 + 2 * NE * KD], rowsln[:, :], K["ident"][0:2 * NE * KD, 0:2 * NE * KD]).then_inc(turned, 1)
            pe.wait_ge(small, 2)
            with pe.Fori(0, NE) as e:
                pe.wait_ge(raw_in[0], 16 * e + 16)
                pe.wait_ge(bias_out, e + 1)
                for m in range(MH):
                    for k in range(KD):
                        mm = pe.matmul(bps[0][:, m:m + 1], stage[:, 0, k * HID + m * P:k * HID + (m + 1) * P],
                                       K["lnb"][:, k, bass.ds(e, 1)], start=(k == 0), stop=(k == KD - 1))
                mm.then_inc(biased, 1)

        @block.scalar
        def _(act):
            act.wait_ge(small, 3)
            with act.Fori(0, NE) as e:
                act.wait_ge(raw_in[0], 16 * e + 16)
                for k in range(KD):
                    act.activation(K["w1"][:, 0, bass.ds(e, 1), k, :].rearrange("p a h -> p (a h)"),
                                   stage[:, 0, k * HID:(k + 1) * HID], ACT.Copy,
                                   scale=K["gain"][:, k, bass.ds(e, 1)]).then_inc(hi, 1)
                act.wait_ge(raw_in[1], 16 * e + 16)
                act.activation(K["w2"][:, 0, bass.ds(e, 1), :, :].rearrange("p a m d -> p (a m d)"),
                               stage[:, 1, :], ACT.Copy, scale=SC).then_inc(hi, 1)

        @block.vector
        def _(dve):
            dve.wait_ge(turned, 1)
            dve.tensor_copy(b1T[:, :, :], tps[:, 0:NE * MH].rearrange("p (e m) -> p e m", m=MH)).then_inc(small, 1)
            dve.tensor_copy(K["lnb"][:, :, :], tps[:, 64 + NE * KD:64 + 2 * NE * KD].rearrange("p (e k) -> p k e", k=KD)).then_inc(small, 1)
            dve.tensor_scalar(K["gain"][:, :, :], tps[:, 64:64 + NE * KD].rearrange("p (e k) -> p k e", k=KD),
                              SC, None, ALU.mult).then_inc(small, 1)
            dve.wait_ge(small, 3)
            dve.sem_inc(lo, 1)
            dve.sem_inc(bias_out, 1)
            with dve.Fori(0, NE) as e:
                for k in range(KD):
                    dve.wait_ge(hi, 3 * e + k + 1)
                    dve.scalar_tensor_tensor(out=K["w1"][:, 1, bass.ds(e, 1), k, :].rearrange("p a h -> p (a h)"),
                                             in0=stage[:, 0, k * HID:(k + 1) * HID], scalar=K["gain"][:, k, bass.ds(e, 1)],
                                             in1=K["w1"][:, 0, bass.ds(e, 1), k, :].rearrange("p a h -> p (a h)"),
                                             op0=ALU.mult, op1=ALU.subtract).then_inc(lo, 1)
                dve.wait_ge(biased, e + 1)
                dve.tensor_tensor(K["b1p"][:, bass.ds(e, 1), :].rearrange("p a m -> p (a m)"), bps[0][:, 0:MH],
                                  b1T[:, bass.ds(e, 1), :].rearrange("p a m -> p (a m)"), ALU.add).then_inc(bias_out, 1)
                dve.wait_ge(hi, 3 * e + 3)
                dve.scalar_tensor_tensor(out=K["w2"][:, 1, bass.ds(e, 1), :, :].rearrange("p a m d -> p (a m d)"),
                                         in0=stage[:, 1, :], scalar=SC,
                                         in1=K["w2"][:, 0, bass.ds(e, 1), :, :].rearrange("p a m d -> p (a m d)"),
                                         op0=ALU.mult, op1=ALU.subtract).then_inc(lo, 1)


def experts(nc, K, xd, yd):
    R, B = 4, 2
    T = EP // P
    with ExitStack() as ctx:
        def sb(name, shape, dt=F32):
            return ctx.enter_context(nc.sbuf_tensor(name, shape, dt))

        def sem(name):
            return ctx.enter_context(nc.semaphore(name))

        ident16 = sb("ident16", [P, P], F16)
        xs = sb("xs", [P, R, T, 2 * D], F16)
        xT = sb("exT", [P, B, 2, KD, EP], F16)
        h = sb("h", [P, MH, EP])
        hp = sb("hparts", [P, 2, B, MH, EP], F16)
        y = sb("y", [P, B, T, D])
        tps = [ctx.enter_context(nc.psum_tensor(f"etps{b}", [P, 1024], F16)) for b in range(B)]
        hps = [ctx.enter_context(nc.psum_tensor(f"hps{b}", [P, 512], F32)) for b in range(4)]
        yps = [ctx.enter_context(nc.psum_tensor(f"yps{b}", [P, 512], F32)) for b in range(T)]
        ident_ready = sem("ident_ready")
        x_in = [sem(f"slots_in{s}") for s in range(R)]
        turned = sem("eturned")
        xT_ready = sem("exT_ready")
        h_ready = sem("h_ready")
        acted = sem("acted")
        h_split = sem("h_split")
        y_ready = sem("y_ready")
        y_out = sem("y_out")
        y_stored = sem("y_stored")
        y_free = sem("y_free")
        block = ctx.enter_context(nc.Block())

        @block.sync
        def _(sp):
            def load(n, s):
                sp.dma_start(xs[:, s, :, :], xd[bass.ds(n * EP, EP), :].rearrange("(t p) d -> p t d", p=P)).then_inc(x_in[s], 16)

            for n in range(R):
                load(n, n)
            sp.sem_inc(y_free, B)
            with sp.Fori(0, ETL // R) as i:
                for s in range(R):
                    n = i * R + s
                    sp.wait_ge(turned, n + 1)
                    load(n + R, s)
                    sp.wait_ge(y_out, 2 * n + 4)
                    sp.dma_start(yd[bass.ds(n * EP, EP), :].rearrange("(t p) d -> p t d", p=P), y[:, s % B, :, :]).then_inc(y_stored, 16)
                    sp.wait_ge(y_stored, 16 * n + 16)
                    sp.sem_inc(y_free, 1)
            for s in range(R):
                sp.wait_ge(x_in[s], 16 * (ETL // R + 1))

        @block.tensor
        def _(pe):
            def turn(s):
                for part in range(2):
                    for k in range(KD):
                        for t in range(T):
                            at = ((part * KD + k) * T + t) * P
                            mm = pe.transpose(tps[s % B][:, at:at + P], xs[:, s % R, t, part * D + k * P:part * D + (k + 1) * P],
                                              ident16[:, :])
                mm.then_inc(turned, 1)

            def layer1(s, e):
                for m in range(MH):
                    out = hps[m // 2][:, (m % 2) * EP:(m % 2 + 1) * EP]
                    terms = [(wp, xp, k) for k in range(KD) for wp, xp in ((0, 0), (0, 1), (1, 0))]
                    for q, (wp, xp, k) in enumerate(terms):
                        mm = pe.matmul(out, K["w1"][:, wp, bass.ds(e, 1), k, m * P:(m + 1) * P].rearrange("p a h -> p (a h)"),
                                       xT[:, s % B, xp, k, :], start=(q == 0), stop=(q == len(terms) - 1))
                    if m % 2 == 1:
                        mm.then_inc(h_ready, 1)

            def layer2(s, e):
                terms = [(m, hpart, wp) for m in range(MH) for hpart, wp in ((0, 0), (1, 0), (0, 1))]
                for q, (m, hpart, wp) in enumerate(terms):
                    for t in range(T):
                        mm = pe.matmul(yps[t][:, 0:D], hp[:, hpart, s % B, m, t * P:(t + 1) * P],
                                       K["w2"][:, wp, bass.ds(e, 1), m, :].rearrange("p a d -> p (a d)"),
                                       start=(q == 0), stop=(q == len(terms) - 1))
                mm.then_inc(y_ready, 1)

            def expert_of(n):
                return pe.value_load(K["erow"][0:1, bass.ds(n, 1)], min_val=0, max_val=NE - 1)

            pe.wait_ge(ident_ready, 1)
            pe.wait_ge(x_in[0], 16)
            turn(0)
            pe.wait_ge(x_in[1], 16)
            turn(1)
            pe.wait_ge(xT_ready, 1)
            layer1(0, expert_of(0))
            with pe.Fori(0, ETL // R) as i:
                for s in range(R):
                    n = i * R + s
                    e_now, e_next = expert_of(n), expert_of(n + 1)
                    pe.wait_ge(xT_ready, n + 2)
                    pe.wait_ge(acted, n * MH + MH)
                    layer1(s + 1, e_next)
                    pe.wait_ge(x_in[(s + 2) % R], 16 * i + 16 * ((s + 2) // R + 1))
                    turn(s + 2)
                    pe.wait_ge(h_split, 4 * n + 4)
                    pe.wait_ge(y_out, 2 * n + 2)
                    layer2(s, e_now)

        @block.scalar
        def _(act):
            def gelu(n, e):
                for m in range(MH):
                    if m % 2 == 0:
                        act.wait_ge(h_ready, 4 * n + m // 2 + 1)
                    act.activation(h[:, m, :], hps[m // 2][:, (m % 2) * EP:(m % 2 + 1) * EP], ACT.Gelu,
                                   bias=K["b1p"][:, bass.ds(e, 1), m], scale=1.0 / SC).then_inc(acted, 1)

            def expert_of(n):
                return act.value_load(K["erow"][0:1, bass.ds(n, 1)], min_val=0, max_val=NE - 1)

            gelu(0, expert_of(0))
            with act.Fori(0, ETL) as n:
                e = expert_of(n + 1)
                act.wait_ge(h_split, 4 * n + 4)
                gelu(n + 1, e)

        @block.vector
        def _(dve):
            def copy_turned(n, s):
                dve.wait_ge(turned, n + 1)
                dve.tensor_copy(xT[:, s % B, :, :, :].rearrange("p a k n -> p (a k n)"), tps[s % B][:, :]).then_inc(xT_ready, 1)

            def split(n, s, half):
                ms = slice(half * MH // 2, (half + 1) * MH // 2)
                dve.wait_ge(acted, n * MH + ms.stop)
                dve.tensor_copy(hp[:, 0, s % B, ms, :], h[:, ms, :]).then_inc(h_split, 1)
                dve.wait_ge(h_split, 4 * n + 2 * half + 1)
                dve.tensor_tensor(hp[:, 1, s % B, ms, :], h[:, ms, :], hp[:, 0, s % B, ms, :], ALU.subtract).then_inc(h_split, 1)

            dve.tensor_copy(ident16[:, :], K["ident"][:, :]).then_inc(ident_ready, 1)
            dve.sem_inc(y_out, 2)
            for n in range(B):
                copy_turned(n, n)
            split(0, 0, 0)
            split(0, 0, 1)
            with dve.Fori(0, ETL // B) as i:
                for s in range(B):
                    n = i * B + s
                    e = dve.value_load(K["erow"][0:1, bass.ds(n, 1)], min_val=0, max_val=NE - 1)
                    split(n + 1, s + 1, 0)
                    copy_turned(n + 2, s + 2)
                    split(n + 1, s + 1, 1)
                    dve.wait_ge(y_free, n + 1)
                    dve.wait_ge(y_ready, n + 1)
                    for t in range(T):
                        dve.scalar_tensor_tensor(out=y[:, s % B, t, :], in0=yps[t][:, 0:D], scalar=1.0 / SC,
                                                 in1=K["b2b"][:, bass.ds(e, 1), :].rearrange("p a d -> p (a d)"),
                                                 op0=ALU.mult, op1=ALU.add).then_inc(y_out, 1)


def combine(nc, K, yd, out):
    C = 7
    with ExitStack() as ctx:
        def sb(name, shape, dt=F32):
            return ctx.enter_context(nc.sbuf_tensor(name, shape, dt))

        def sem(name):
            return ctx.enter_context(nc.semaphore(name))

        idx = sb("cidx", [P, 2, C], I32)
        yy = sb("yy", [P, C, 2, D])
        xo = sb("xo", [P, 2 * C, D])
        idx_ready = sem("cidx_ready")
        landed = [sem(f"y_landed{j}") for j in range(C)]
        mixed = sem("mixed")
        x2_in = [sem(f"x2_in{s}") for s in range(2)]
        stored = [sem(f"out_stored{s}") for s in range(2)]
        begun = sem("combine_begun")
        block = ctx.enter_context(nc.Block())

        @block.gpsimd
        def _(pool):
            with pool.Fori(0, NT // C) as c:
                for j in range(C):
                    pool.wait_ge(idx_ready, c * C + j + 1)
                    pool.sem_inc(begun, 1)
                    for k in range(2):
                        pool.indirect_dma_start(
                            out=yy[:, j, k, :], out_offset=None, in_=yd[:, :],
                            in_offset=bass.IndirectOffsetOnAxis(ap=idx[:, k, j:j + 1], axis=0)).then_inc(landed[j], 16)

        @block.vector
        def _(dve):
            for j in range(C):
                dve.tensor_copy(idx[:, :, j], K["slot"][:, :, j]).then_inc(idx_ready, 1)

            def mix(c, half):
                dve.wait_ge(x2_in[half], (c // 2) * 16 + 16 if isinstance(c, int) else c * 8 + 16 - 8 * half)
                for j in range(C):
                    t = c * C + j
                    tile = xo[:, half * C + j, :]
                    dve.wait_ge(landed[j], 32 * c + 32)
                    for k in range(2):
                        dve.scalar_tensor_tensor(out=tile, in0=yy[:, j, k, :], scalar=K["gate"][:, k, bass.ds(t, 1)], in1=tile,
                                                 op0=ALU.mult, op1=ALU.add).then_inc(mixed, 1)
                        dve.wait_ge(mixed, 2 * t + k + 1)
                    dve.tensor_copy(idx[:, :, j], K["slot"][:, :, bass.ds(t + C, 1)].rearrange("p k a -> p (k a)")).then_inc(idx_ready, 1)

            with dve.Fori(0, NT // C - 1, 2) as c:
                mix(c, 0)
                mix(c + 1, 1)
            mix(NT // C - 1, 0)

        @block.sync
        def _(sp):
            def rows(dram, c):
                return dram[bass.ds(c * (C * P), C * P), :].rearrange("(t p) d -> p t d", p=P)

            def load(c, half):
                sp.dma_start(xo[:, half * C:(half + 1) * C, :], rows(K["x2d"], c)).then_inc(x2_in[half], 16)

            load(0, 0)
            load(1, 1)
            for c in range(NT // C - 1):
                sp.wait_ge(mixed, 2 * C * c + 2 * C)
                sp.dma_start(rows(out, c), xo[:, (c % 2) * C:(c % 2 + 1) * C, :]).then_inc(stored[c % 2], 16)
                if c + 2 < NT // C:
                    sp.wait_ge(stored[c % 2], 16 * (c // 2 + 1))
                    load(c + 2, c % 2)
            sp.wait_ge(mixed, 2 * NT)
            sp.dma_start(out[(NT - C) * P:(NT - 1) * P, :].rearrange("(t p) d -> p t d", p=P),
                         xo[:, 0:C - 1, :]).then_inc(stored[0], 16)
            sp.dma_start(out[(NT - 1) * P:NODES, :], xo[0:TAIL, C - 1, :]).then_inc(stored[0], 16)
            sp.wait_ge(stored[0], 16 * 5)
            sp.wait_ge(stored[1], 16 * 3)





def build(nc, x, src, dst, gnn_W, gnn_att, Wr, br, ln_g, ln_b, W1, b1, W2, b2, out):
    def scratch(name, shape, dt=F32):
        return nc.dram_tensor(name, shape, dt).ap()

    zt = scratch("zt", [NT * P, D])
    es_tab = scratch("es_tab", [NT * P, HEADS])
    ed_edge = scratch("ed_edge", [(EC + NT) * P, HEADS])
    rec = scratch("rec", [6, P * EC])
    wtab = scratch("wtab", [VB * P], I32)
    xd = scratch("xd", [XTL * EP, 2 * D], F16)
    yd = scratch("yd", [ETL * EP, D])
    with ExitStack() as ctx:
        def sb(name, shape, dt=F32):
            return ctx.enter_context(nc.sbuf_tensor(name, shape, dt))

        K = {"ident": sb("ident", [P, P]), "ones": sb("ones", [P, P]), "iota": sb("iota", [P, P]),
             "mean": sb("mean", [P, NT]), "rstd": sb("rstd2", [P, NT]), "gate": sb("gate", [P, 2, NT]),
             "slot": sb("slot", [P, 2, NT + 7], I32), "erow": sb("erow", [1, P], I32),
             "x2d": scratch("x2d", [NT * P, D]), "ends_at": [], "carried_at": []}
        constants(nc, K)
        with ExitStack() as nodes:
            K["x2"] = nodes.enter_context(nc.sbuf_tensor("x2", [P, NT, D], F32))
            with ExitStack() as gnn:
                K["att_node"] = gnn.enter_context(nc.sbuf_tensor("att_node", [P, NT, 2 * HEADS], F32))
                project_nodes(nc, K, x, gnn_W, gnn_att, zt, es_tab, ed_edge)
                K["start"] = gnn.enter_context(nc.sbuf_tensor("start", [P, NT + 1], F32))
                edge_scores(nc, K, src, dst, es_tab, ed_edge, rec, xd, scratch("lo_rows", [P * EC], BF16))
                for name, shape, dt in (("srcV", [P, VB * P], I32), ("dstV", [P, VB * P], F32),
                                        ("exV", [P, VB * P, HEADS], F32), ("wrow", [1, VB * P], I32)):
                    K[name] = gnn.enter_context(nc.sbuf_tensor(name, shape, dt))
                plan_visits(nc, K, rec, wtab)
                aggregate(nc, K, zt)
            route(nc, K, Wr, br, xd)
            dispatch(nc, K, xd)
        with ExitStack() as ffn:
            for name, shape, dt in (("w1", [P, 2, NE, KD, HID], F16), ("w2", [P, 2, NE, MH, D], F16), ("b1p", [P, NE, MH], F32),
                                    ("b2b", [P, NE, D], F32), ("gain", [P, KD, NE], F32), ("lnb", [P, KD, NE], F32)):
                K[name] = ffn.enter_context(nc.sbuf_tensor(name + "_keep", shape, dt))
            prepare_weights(nc, K, ln_g, ln_b, W1, b1, W2, b2)
            experts(nc, K, xd, yd)
        combine(nc, K, yd, out)


_INS = ["x", "src", "dst", "L0_gnn_W", "L0_gnn_att", "L0_ffn_Wr", "L0_ffn_br", "L0_ffn_ln_g", "L0_ffn_ln_b",
        "L0_ffn_W1", "L0_ffn_b1", "L0_ffn_W2", "L0_ffn_b2"]


def kernel(**inputs):
    import numpy as _np
    import concourse.bacc as _bacc
    from concourse import mybir as _mybir
    from concourse.bass_utils import run_bass_kernel_spmd as _run

    nc = _bacc.Bacc("TRN2", target_bir_lowering=False, num_devices=1)
    arrays, args = {}, []
    for name in _INS:
        a = _np.ascontiguousarray(inputs[name])
        arrays[f"in_{name}_dram"] = a
        args.append(nc.dram_tensor(f"in_{name}_dram", a.shape, _mybir.dt.from_np(a.dtype), kind="ExternalInput").ap())
    args.append(nc.dram_tensor("out_0_dram", (NODES, D), _mybir.dt.float32, kind="ExternalOutput").ap())
    build(nc, *args)
    r = _run(nc, [arrays], core_ids=[0])
    return r.results[0]["out_0_dram"]
```
